# Optimizing a Trainium2 kernel written in Bass

```python
import numpy as np
import jax
import jax.numpy as jnp

def _softmax(x, axis=-1):
    return jax.nn.softmax(x, axis=axis)

def _gelu(x):
    return jax.nn.gelu(x, approximate=True)

def _silu(x):
    return jax.nn.silu(x)

def _sigmoid(x):
    return jax.nn.sigmoid(x)

def _layernorm(x, axis=-1, eps=1e-05):
    m = jnp.mean(x, axis=axis, keepdims=True)
    v = jnp.var(x, axis=axis, keepdims=True)
    return (x - m) / jnp.sqrt(v + eps)

def _scatter_add(tgt, idx, src, axis=0):
    return tgt.at[idx].add(src)

def _segment_sum(src, seg, n):
    return jax.ops.segment_sum(src, seg, n)
kernel_name = 'mk_sandwich_d1_jaxref_r8_8aa103'

def setup_inputs(seed: int=0):
    np.random.seed(seed)
    _w = jnp.asarray

    def _L0_attn_setup():
        import jax, jax.numpy as jnp
        import numpy as np
        B, N, D = (2, 256, 128)
        H, QH, DH = (8, 16, 64)
        SOFTCLAMP = 50.0

        def _rmsnorm(x, w):
            eps = jnp.finfo(x.dtype).eps
            return x * jax.lax.rsqrt(jnp.mean(x * x, axis=-1, keepdims=True) + eps) * w

        def _l2norm(x):
            n = jnp.maximum(jnp.linalg.norm(x, axis=-1, keepdims=True), 1e-12)
            return x / n

        def _mh_rmsnorm(x, gamma):
            scale = (gamma + 1.0) * np.sqrt(x.shape[-1]).astype(np.float32)
            return _l2norm(x) * scale[None, :, None, :]
        key = jax.random.key(seed)
        ks = jax.random.split(key, 7)
        return {'tokens': jax.random.normal(ks[0], (B, N, D), jnp.float32), 'norm_w': jnp.ones((D,), jnp.float32) + 0.02 * jax.random.normal(ks[1], (D,), jnp.float32), 'Wq': 0.02 * jax.random.normal(ks[2], (D, QH * DH), jnp.float32), 'Wkv': 0.02 * jax.random.normal(ks[3], (D, 2 * H * DH), jnp.float32), 'Wout': 0.02 * jax.random.normal(ks[4], (H * DH, D), jnp.float32), 'q_gamma': 0.02 * jax.random.normal(ks[5], (QH, DH), jnp.float32), 'k_gamma': 0.02 * jax.random.normal(ks[6], (H, DH), jnp.float32)}
    _L0_attn_in = _L0_attn_setup()

    def _L0_ffn_setup():
        import jax, jax.numpy as jnp
        import numpy as np
        B, N, D = (4, 256, 128)
        SPARSITY = 0.01
        key = jax.random.key(seed)
        k1, k2, k3 = jax.random.split(key, 3)
        x = jax.random.normal(k1, (B, N, D), dtype=jnp.float32)
        spatial = jax.random.normal(k2, (D, D), dtype=jnp.float32) * 0.02
        freq = jnp.fft.fft(spatial, axis=-1)
        k = int(D * SPARSITY)
        mag = jnp.abs(freq)
        kth = jax.lax.top_k(mag, k)[0][:, -1:]
        w_sparse = jnp.where(mag >= kth, freq, 0.0 + 0j)
        bias = jax.random.normal(k3, (D,), dtype=jnp.float32) * 0.01
        return {'x': x, 'w_freq_real': jnp.real(w_sparse).astype(jnp.float32), 'w_freq_imag': jnp.imag(w_sparse).astype(jnp.float32), 'bias': bias}
    _L0_ffn_in = _L0_ffn_setup()
    _d = {'L0_attn_tokens': _L0_attn_in['tokens'], 'L0_attn_norm_w': _L0_attn_in['norm_w'], 'L0_attn_Wq': _L0_attn_in['Wq'], 'L0_attn_Wkv': _L0_attn_in['Wkv'], 'L0_attn_Wout': _L0_attn_in['Wout'], 'L0_attn_q_gamma': _L0_attn_in['q_gamma'], 'L0_attn_k_gamma': _L0_attn_in['k_gamma'], 'L0_ffn_w_freq_real': _L0_ffn_in['w_freq_real'], 'L0_ffn_w_freq_imag': _L0_ffn_in['w_freq_imag'], 'L0_ffn_bias': _L0_ffn_in['bias']}
    _x0 = _d['L0_attn_tokens']
    _d['L0_attn_tokens'] = jax.random.normal(jax.random.fold_in(jax.random.key(seed), 1), (8, 512, 128), dtype=_x0.dtype)
    del _x0
    return _d

def reference(L0_attn_tokens, L0_attn_norm_w, L0_attn_Wq, L0_attn_Wkv, L0_attn_Wout, L0_attn_q_gamma, L0_attn_k_gamma, L0_ffn_w_freq_real, L0_ffn_w_freq_imag, L0_ffn_bias):

    def _L0_attn_ref(tokens, norm_w, Wq, Wkv, Wout, q_gamma, k_gamma):
        import jax, jax.numpy as jnp
        import numpy as np
        B, N, D = (2, 256, 128)
        H, QH, DH = (8, 16, 64)
        SOFTCLAMP = 50.0

        def _rmsnorm(x, w):
            eps = jnp.finfo(x.dtype).eps
            return x * jax.lax.rsqrt(jnp.mean(x * x, axis=-1, keepdims=True) + eps) * w

        def _l2norm(x):
            n = jnp.maximum(jnp.linalg.norm(x, axis=-1, keepdims=True), 1e-12)
            return x / n

        def _mh_rmsnorm(x, gamma):
            scale = (gamma + 1.0) * np.sqrt(x.shape[-1]).astype(np.float32)
            return _l2norm(x) * scale[None, :, None, :]
        b, n, d = tokens.shape
        x = _rmsnorm(tokens, norm_w)
        q = (x @ Wq).reshape(b, n, QH, DH).transpose(0, 2, 1, 3)
        kv = x @ Wkv
        k = kv[..., :H * DH].reshape(b, n, H, DH).transpose(0, 2, 1, 3)
        v = kv[..., H * DH:].reshape(b, n, H, DH).transpose(0, 2, 1, 3)
        q = _mh_rmsnorm(q, q_gamma)
        k = _mh_rmsnorm(k, k_gamma)
        g = QH // H
        q = q.reshape(b, H, g, n, DH)
        sim = jnp.einsum('bhgid,bhjd->bhgij', q, k)
        sim = jnp.tanh(sim / SOFTCLAMP) * SOFTCLAMP
        sim = sim * DH ** (-0.5)
        neg = -jnp.finfo(sim.dtype).max
        causal = jnp.triu(jnp.ones((n, n), dtype=bool), 1)
        sim = jnp.where(causal, neg, sim)
        attn = jax.nn.softmax(sim, axis=-1)
        out = jnp.einsum('bhgij,bhjd->bhid', attn, v)
        out = out.transpose(0, 2, 1, 3).reshape(b, n, H * DH)
        return out @ Wout

    def _L0_ffn_ref(x, w_freq_real, w_freq_imag, bias):
        import jax, jax.numpy as jnp
        import numpy as np
        B, N, D = (4, 256, 128)
        SPARSITY = 0.01
        w = jax.lax.complex(w_freq_real, w_freq_imag)
        x_freq = jnp.fft.fft(x, axis=-1)
        y_freq = jnp.einsum('bnd,do->bno', x_freq, w)
        y = jnp.real(jnp.fft.ifft(y_freq, axis=-1))
        return y + bias
    x = L0_attn_tokens
    x = x + _layernorm(_L0_attn_ref(_layernorm(x, axis=-1), L0_attn_norm_w, L0_attn_Wq, L0_attn_Wkv, L0_attn_Wout, L0_attn_q_gamma, L0_attn_k_gamma), axis=-1)
    x = x + _layernorm(_L0_ffn_ref(_layernorm(x, axis=-1), L0_ffn_w_freq_real, L0_ffn_w_freq_imag, L0_ffn_bias), axis=-1)
    return x

_drawn_inputs = setup_inputs


def setup_inputs(seed=0):
    import zlib

    import numpy as np

    out = dict(_drawn_inputs(seed))
    spreads = {}
    factors = {'L0_attn_q_gamma': 4.608, 'L0_attn_k_gamma': 4.689, 'L0_ffn_bias': 4.166}
    for name, (base, spread) in spreads.items():
        noise = np.random.default_rng([zlib.crc32(name.encode()), seed]).standard_normal(out[name].shape)
        drawn = base * np.exp(spread * noise) if base else spread * noise
        out[name] = jnp.asarray(drawn.astype(out[name].dtype))
    for name, factor in factors.items():
        out[name] = (out[name] * factor).astype(out[name].dtype)
    return out
```

```python
import concourse.bass as bass
from concourse import mybir
from contextlib import ExitStack

FP32 = mybir.dt.float32
ALU = mybir.AluOpType
ACT = mybir.ActivationFunctionType
AX = mybir.AxisListType

P = 128
B, N, D = 8, 512, 128
KH, G, DH = 8, 2, 64
T = N // P
QW, KW = KH * G * DH, KH * DH
EPS_LN, EPS_RMS = 1e-5, 1.1920928955078125e-07
SOFTCLAMP = 50.0
UNITS = 3
P_AT = [[0, 512], [1024, 1408], [1792, 2176], [2048, 2432]]
P_LEN = 2560
PJ, TR = 4, 4


def wait(eng, sem, value):
    if isinstance(value, int) and value <= 0:
        return
    eng.wait_ge(sem, value)


def wait_apart(eng, sem, value, steps):
    wait(eng, sem, value)
    if not isinstance(value, int):
        eng.sem_inc(steps, 1)


def min_batch(n):
    return min(n, B) if isinstance(n, int) else n


def build(nc, x, norm_w, wq, wkv, wout, q_gamma, k_gamma, w_real, w_imag, bias, dft, out):
    x_t = x.rearrange("b (t p) d -> b p t d", p=P)
    out_t = out.rearrange("b (t p) d -> b p t d", p=P)
    ctx = ExitStack()
    with ctx:
        def sb(name, shape):
            return ctx.enter_context(nc.sbuf_tensor(name, shape, FP32))

        def sem(name):
            return ctx.enter_context(nc.semaphore(name))

        w_all = sb("w_all", [P, QW + 2 * KW])
        w_out = sb("w_out", [P, 4, D])
        nw_col = sb("nw_col", [P, 1])
        tables = sb("tables", [P, 3, P])
        wf = sb("wf", [P, 2, P])
        a_t = sb("a_t", [P, 2, P])
        mix = sb("mix", [P, P])
        bias_row = sb("bias_row", [1, P])
        bias_all = sb("bias_all", [P, P])
        ones_row = sb("ones_row", [1, P])
        ident = sb("ident", [P, P])
        gq8 = sb("gq8", [KH, G, DH])
        gk8 = sb("gk8", [KH, G, DH])
        gk8p = sb("gk8p", [KH, G, DH])
        g8 = sb("g8", [KH, G * DH])
        gain = sb("gain", [P, KH])
        minus_half = sb("minus_half", [P, 24])
        xin = [sb(f"xin{i}", [P, T, D]) for i in range(2)]
        xn = sb("xn", [P, T, D])
        xT = sb("xT", [P, T * P])
        st1 = sb("st1", [P, T, 6]); mv1 = sb("mv1", [P, T, 2]); ve1 = sb("ve1", [P, T]); rs1 = sb("rs1", [P, T])
        raw = [sb(f"raw{i}", [P, QW + KW]) for i in range(2)]
        sq = sb("sq", [P, QW + KW])
        ssq = [sb(f"ssq{i}", [P, 24]) for i in range(2)]
        ssg = sb("ssg", [P, 24])
        rn = [sb(f"rn{i}", [P, 24]) for i in range(2)]
        qn = [sb(f"qn{i}", [P, QW + 2 * KW]) for i in range(2)]
        qT = [sb(f"qT{i}", [P, KH, N]) for i in range(2)]
        kT = [sb(f"kT{i}", [P, KH, N]) for i in range(2)]
        vt = [sb(f"vt{i}", [P, T, KH, DH + 1]) for i in range(2)]
        prob = [sb(f"prob{i}", [P, P_LEN]) for i in range(2)]
        rden = sb("rden", [P, G, T])
        og = sb("og", [P, G, T, DH])
        otok = [sb(f"otok{i}", [P, T, KW]) for i in range(2)]
        oT = sb("oT", [P, T, 4, P])
        attn = sb("attn", [P, T, D])
        xres = sb("xres", [P, T, D])
        z2 = sb("z2", [P, T, D])
        x1 = sb("x1", [P, T, D])
        xn3 = sb("xn3", [P, T, D])
        x3T = sb("x3T", [P, T * P])
        y = sb("y", [P, T, D])
        z4 = sb("z4", [P, T, D])
        res = sb("res", [P, T, D])
        ln = [[sb(f"ln{k}_{i}", [P, T, w] if w > 1 else [P, T]) for i, w in enumerate((6, 2, 1, 1))]
              for k in range(3)]

        score = [ctx.enter_context(nc.psum_tensor(f"score{i}", [P, 2, 512], FP32)) for i in range(2)]
        acc = ctx.enter_context(nc.psum_tensor("acc", [P, G, 512], FP32))
        bank = [ctx.enter_context(nc.psum_tensor(f"bank{i}", [P, 512], FP32)) for i in range(2)]
        acc_o = acc[:, :, 0:T * (DH + 1)].rearrange("p g (t c) -> p g t c", c=DH + 1)

        s_const = sem("s_const"); s_setup = sem("s_setup"); s_gp = sem("s_gp"); s_pe0 = sem("s_pe0")
        s_w = sem("s_w"); s_tab = sem("s_tab"); s_g = sem("s_g")
        ve_steps = sem("ve_steps"); gp_steps = sem("gp_steps")
        x_loaded = [sem("x_even_loaded"), sem("x_odd_loaded")]; r_loaded = sem("r_loaded"); res_free = sem("res_free")
        st_done = [sem(f"st{k}_done") for k in range(4)]
        mv_done = [sem(f"mv{k}_done") for k in range(4)]
        ve_done = [sem(f"ve{k}_done") for k in range(4)]
        rs_done = [sem(f"rs{k}_done") for k in range(4)]
        xn_done = sem("xn_done"); xt_done = sem("xt_done"); xt_copied = sem("xt_copied")
        pj_done = sem("pj_done"); pj_copied = sem("pj_copied")
        sq_done = sem("sq_done"); ssq_done = sem("ssq_done"); ssg_done = sem("ssg_done")
        rn_done = sem("rn_done"); qn_done = sem("qn_done")
        tr_done = sem("tr_done"); qT_ready = sem("qT_ready"); kT_ready = sem("kT_ready")
        s_done = sem("s_done"); tanh_done = sem("tanh_done"); exp_done = sem("exp_done")
        mask_done = sem("mask_done"); av_done = sem("av_done")
        rden_done = sem("rden_done"); og_done = sem("og_done"); o_done = sem("o_done")
        ot_done = sem("ot_done"); ot_copied = sem("ot_copied"); op_done = sem("op_done")
        op_copied = sem("op_copied"); z2_done = sem("z2_done"); x1_done = sem("x1_done")
        xn3_done = sem("xn3_done"); ft_done = sem("ft_done"); ft_copied = sem("ft_copied")
        ff_done = sem("ff_done"); y_done = sem("y_done"); z4_done = sem("z4_done")
        res_done = sem("res_done")

        block = ctx.enter_context(nc.Block())

        def batches(eng, iteration):
            iteration(0, 0, True, False)
            with eng.Fori(1, B - 1, 2) as b:
                iteration(b, 1, True, True)
                iteration(b + 1, 0, True, True)
            iteration(B - 1, (B - 1) % 2, False, True)

        @block.sync
        def _(sp):
            sp.sem_inc(res_free, 16)
            sp.dma_start(xin[0][:], x_t[0]).then_inc(x_loaded[0], 16)
            sp.dma_start(w_all[:, 0:QW], wq).then_inc(s_w, 16)
            sp.dma_start(w_all[:, QW:], wkv).then_inc(s_w, 16)
            sp.dma_start(nw_col[:], norm_w.rearrange("(d o) -> d o", o=1)).then_inc(s_w, 16)
            sp.dma_start(xin[1][:], x_t[1]).then_inc(x_loaded[1], 16)
            sp.dma_start(gq8[:], q_gamma.rearrange("(h g) d -> h g d", g=G)).then_inc(s_g, 16)
            for g in range(G):
                sp.dma_start(gk8[:, g, :], k_gamma).then_inc(s_g, 16)
            sp.dma_start(w_out[:], wout.rearrange("(c p) d -> p c d", p=P)).then_inc(s_tab, 16)
            sp.dma_start(tables[:], dft.rearrange("k p d -> p k d")).then_inc(s_tab, 16)
            sp.dma_start(wf[:, 0, :], w_real).then_inc(s_tab, 16)
            sp.dma_start(wf[:, 1, :], w_imag).then_inc(s_tab, 16)
            sp.dma_start(bias_row[:], bias.rearrange("(o d) -> o d", o=1)).then_inc(s_tab, 16)

            def load_next(b, par):
                wait(sp, xn_done, T * (b + 1))
                sp.dma_start(xin[par][:], x_t[b + 2]).then_inc(x_loaded[par], 16)

            def load_residual(b):
                wait(sp, x1_done, b)
                sp.dma_start(xres[:], x_t[b]).then_inc(r_loaded, 16)

            def store(p):
                wait(sp, res_done, p + 1)
                sp.dma_start(out_t[p], res[:]).then_inc(res_free, 16)

            def iteration(b, par, prep):
                if prep:
                    load_next(b, par)
                load_residual(b)
                if not (isinstance(b, int) and b == 0):
                    store(b - 1)

            iteration(0, 0, True)
            with sp.Fori(1, B - 3, 2) as b:
                iteration(b, 1, True)
                iteration(b + 1, 0, True)
            iteration(B - 3, 1, True)
            iteration(B - 2, 0, False)
            iteration(B - 1, 1, False)
            store(B - 1)
            sp.wait_ge(res_free, 16 * (B + 1))

        @block.tensor
        def _(pe):
            def setup():
                pe.wait_ge(s_const, 3)
                pe.wait_ge(s_setup, 3)
                pe.transpose(bank[0][:, 0:KH], g8[:], ident[0:KH, 0:KH]).then_inc(s_pe0, 1)
                pe.wait_ge(s_tab, 80)
                cos, sin, msin = (tables[:, k, :] for k in range(3))
                wr, wi = wf[:, 0, :], wf[:, 1, :]
                pe.matmul(bank[1][:, 0:P], wr, cos, start=True, stop=False)
                pe.matmul(bank[1][:, 0:P], wi, sin, start=False, stop=True)
                pe.matmul(bank[1][:, P:2 * P], wi, cos, start=True, stop=False)
                pe.matmul(bank[1][:, P:2 * P], wr, msin, start=False, stop=True).then_inc(s_pe0, 1)
                pe.wait_ge(s_setup, 4)
                pe.matmul(bank[0][:, 0:P], ones_row[:], bias_row[:], start=True, stop=True).then_inc(s_pe0, 1)
                pe.wait_ge(s_setup, 6)
                pe.matmul(bank[1][:, 0:P], a_t[:, 0, :], cos, start=True, stop=False)
                pe.matmul(bank[1][:, 0:P], a_t[:, 1, :], msin, start=False, stop=True).then_inc(s_pe0, 1)

            def x_transpose(nb):
                wait(pe, kT_ready, 8 * nb - 1)
                wait(pe, xn_done, T * (nb + 1))
                for t in range(T):
                    mm = pe.transpose(bank[0][:, t * P:(t + 1) * P], xn[:, t, :], ident[:])
                mm.then_inc(xt_done, 1)

            def project(nb, t, post):
                n = T * nb + t
                if t == 0:
                    wait(pe, xt_copied, nb + 1)
                for c in range(PJ):
                    if c >= 2 or t in (1, 2):
                        wait(pe, pj_copied, PJ * n + c - 1)
                    elif t == 0 and post:
                        wait(pe, *((ot_copied, T * (nb - 1)), (op_copied, nb - 1))[c])
                    elif t == 0:
                        wait(pe, kT_ready, 8 * nb - 1 + c)
                    elif post:
                        wait(pe, *((ft_copied, nb - 1), (y_done, nb - 1))[c])
                    else:
                        wait(pe, kT_ready, 2 * (n - 3) + 1 + c)
                    pe.matmul(bank[c % 2][:], xT[:, t * P:(t + 1) * P], w_all[:, c * 512:(c + 1) * 512],
                              start=True, stop=True).then_inc(pj_done, 1)

            def transposes(nb, t):
                n = T * nb + t
                wait(pe, qn_done, 3 * (n + 1))
                for c in range(TR):
                    if c >= 2:
                        wait(pe, qT_ready, 2 * n + c - 1)
                    elif t < 2:
                        wait(pe, pj_copied, PJ * (n + 2) + 3 + c)
                    else:
                        wait(pe, kT_ready, 2 * (n - 1) + 1 + c)
                    for k in range(4):
                        src = qn[t % 2][:, (4 * c + k) * P:(4 * c + k + 1) * P]
                        mm = pe.transpose(bank[c % 2][:, k * P:(k + 1) * P], src, ident[:])
                    mm.then_inc(tr_done, 1)

            def scores(b, par, h, u):
                q = KH * b + h
                if h == 0 and u == 0:
                    wait(pe, qT_ready, 8 * (b + 1))
                    wait(pe, kT_ready, 8 * (b + 1))
                wait(pe, tanh_done, UNITS * q + u - 1)
                s = score[(UNITS * h + u) % 2]
                for j, at in (((0, 0),), ((1, 0),), ((2, 0), (3, 256)))[u]:
                    for g in range(G):
                        row = slice(g * DH, (g + 1) * DH)
                        mm = pe.matmul(s[:, g, at:at + N - j * P], kT[par][row, h, j * P:(j + 1) * P],
                                       qT[par][row, h, j * P:N], start=True, stop=True)
                mm.then_inc(s_done, 1)

            def values(b, par, h):
                q = KH * b + h
                if h == 0:
                    wait(pe, pj_copied, 16 * (b + 1))
                wait(pe, mask_done, 3 * (q + 1))
                wait(pe, og_done, q)
                for g in range(G):
                    for t in range(T):
                        for j in range(t + 1):
                            at = P_AT[j][g] + (t - j) * P
                            mm = pe.matmul(acc[:, g, t * (DH + 1):(t + 1) * (DH + 1)],
                                           prob[h % 2][:, at:at + P], vt[par][:, j, h, :],
                                           start=(j == 0), stop=(j == t))
                mm.then_inc(av_done, 1)

            def o_transposes(p, par):
                wait(pe, o_done, KH * (p + 1))
                for t in range(T):
                    if t == 0:
                        wait(pe, kT_ready, 8 * min_batch(p + 2))
                    elif t == 1:
                        wait(pe, xt_copied, min_batch(p + 3))
                    else:
                        wait(pe, ot_copied, T * p + t - 1)
                    for c in range(4):
                        mm = pe.transpose(bank[1 - t % 2][:, c * P:(c + 1) * P],
                                          otok[par][:, t, c * P:(c + 1) * P], ident[:])
                    mm.then_inc(ot_done, 1)

            def out_project(p):
                wait(pe, ot_copied, T * (p + 1))
                for t in range(T):
                    for c in range(4):
                        mm = pe.matmul(bank[1][:, t * P:(t + 1) * P], oT[:, t, c, :], w_out[:, c, :],
                                       start=(c == 0), stop=(c == 3))
                mm.then_inc(op_done, 1)

            def f_transpose(p, prep):
                wait(pe, xn3_done, T * (p + 1))
                if prep:
                    wait(pe, kT_ready, 8 * (p + 2) + 1)
                for t in range(T):
                    mm = pe.transpose(bank[0][:, t * P:(t + 1) * P], xn3[:, t, :], ident[:])
                mm.then_inc(ft_done, 1)

            def f_mix(p, prep):
                wait(pe, ft_copied, p + 1)
                if prep:
                    wait(pe, kT_ready, 8 * (p + 2) + 2)
                for t in range(T):
                    mm = pe.matmul(bank[1][:, t * P:(t + 1) * P], x3T[:, t * P:(t + 1) * P], mix[:],
                                   start=True, stop=True)
                mm.then_inc(ff_done, 1)

            def iteration(b, par, prep, post):
                for h in range(KH):
                    scores(b, par, h, 0)
                    scores(b, par, h, 1)
                    if h == 1:
                        if prep:
                            x_transpose(b + 1)
                        if post:
                            o_transposes(b - 1, 1 - par)
                            out_project(b - 1)
                    if prep and h in (2, 3, 4):
                        project(b + 1, h - 2, post)
                    if prep and h == 4:
                        transposes(b + 1, 0)
                    if post and h == 4:
                        f_transpose(b - 1, prep)
                    if post and h == 5:
                        f_mix(b - 1, prep)
                    if prep and h == 5:
                        project(b + 1, 3, post)
                    if prep and h >= 5:
                        transposes(b + 1, h - 4)
                    scores(b, par, h, 2)
                    if h >= 1:
                        values(b, par, h - 1)
                    elif post:
                        values(b - 1, 1 - par, KH - 1)

            setup()
            pe.wait_ge(s_setup, 8)
            x_transpose(0)
            for t in range(3):
                project(0, t, False)
            transposes(0, 0)
            project(0, 3, False)
            for t in range(1, T):
                transposes(0, t)
            batches(pe, iteration)
            values(B - 1, (B - 1) % 2, KH - 1)
            o_transposes(B - 1, (B - 1) % 2)
            out_project(B - 1)
            f_transpose(B - 1, False)
            f_mix(B - 1, False)

        @block.scalar
        def _(act):
            def x_copy(nb):
                wait(act, xt_done, nb + 1)
                wait(act, pj_done, 16 * nb)
                act.copy(xT[:], bank[0][:]).then_inc(xt_copied, 1)

            def p_copy(nb, npar, t):
                n = T * nb + t
                for c in range(PJ):
                    wait(act, pj_done, PJ * n + c + 1)
                    if c == 0:
                        wait(act, qn_done, 3 * (n - 1))
                    if c < 3:
                        act.copy(raw[t % 2][:, c * 512:(c + 1) * 512], bank[c % 2][:]).then_inc(pj_copied, 1)
                    else:
                        wait(act, av_done, KH * (nb - 1))
                        act.copy(vt[npar][:, t, :, 0:DH], bank[1][:].rearrange("p (h d) -> p h d", d=DH))\
                           .then_inc(pj_copied, 1)

            def k_copy(nb, npar, t):
                n = T * nb + t
                for c in (2, 3):
                    wait(act, tr_done, TR * n + c + 1)
                    if c == 2:
                        wait(act, s_done, 24 * (nb - 1))
                    h = 4 * (c - 2)
                    act.copy(kT[npar][:, h:h + 4, t * P:(t + 1) * P],
                             bank[c % 2][:].rearrange("p (h n) -> p h n", n=P)).then_inc(kT_ready, 1)

            def tanh(b, h, u):
                q = KH * b + h
                if u == 0:
                    wait(act, av_done, q - 1)
                wait(act, s_done, UNITS * q + u + 1)
                w = 512 if u == 0 else 384
                at = P_AT[u][0]
                act.activation(prob[h % 2][:, at:at + 2 * w].rearrange("p (g n) -> p g n", g=G),
                               score[(UNITS * h + u) % 2][:, :, 0:w], ACT.Tanh,
                               scale=float(DH) / SOFTCLAMP).then_inc(tanh_done, 1)

            def exp(b, h):
                q = KH * b + h
                wait(act, tanh_done, UNITS * (q + 1))
                act.activation(prob[h % 2][:], prob[h % 2][:], ACT.Exp,
                               scale=SOFTCLAMP * DH ** -0.5).then_inc(exp_done, 1)

            def iteration(b, par, prep, post):
                for h in range(KH):
                    tanh(b, h, 0)
                    tanh(b, h, 1)
                    if h == 1 and prep:
                        x_copy(b + 1)
                    if h == 2 and post:
                        attn_copy(b - 1)
                    if prep and 2 <= h <= 4:
                        p_copy(b + 1, 1 - par, h - 2)
                    if prep and h == 4:
                        k_copy(b + 1, 1 - par, 0)
                    if post and h == 5:
                        f_copy(b - 1)
                    if prep and h == 5:
                        p_copy(b + 1, 1 - par, 3)
                    if prep and h >= 5:
                        k_copy(b + 1, 1 - par, h - 4)
                    tanh(b, h, 2)
                    exp(b, h)

            def attn_copy(p):
                wait(act, op_done, p + 1)
                act.copy(attn[:].rearrange("p t d -> p (t d)"), bank[1][:]).then_inc(op_copied, 1)

            def f_copy(p):
                wait(act, ft_done, p + 1)
                act.copy(x3T[:], bank[0][:]).then_inc(ft_copied, 1)

            x_copy(0)
            for t in range(3):
                p_copy(0, 0, t)
            k_copy(0, 0, 0)
            p_copy(0, 0, 3)
            for t in range(1, T):
                k_copy(0, 0, t)
            batches(act, iteration)
            attn_copy(B - 1)
            f_copy(B - 1)

        @block.gpsimd
        def _(gp):
            gp.memset(ident[:], 0.0).then_inc(s_gp, 1)
            gp.wait_ge(s_gp, 1)
            gp.affine_select(out=ident[:], in_=ident[:], compare_op=ALU.not_equal, fill=1.0, base=0,
                             pattern=[[-1, P]], channel_multiplier=1).then_inc(s_const, 1)
            gp.memset(minus_half[:], -0.5).then_inc(s_const, 1)
            gp.memset(ones_row[:], 1.0).then_inc(s_const, 1)
            for i in range(2):
                gp.memset(vt[i][:, :, :, DH:DH + 1], 1.0).then_inc(s_const, 1)

            def rstd(k, batch, ve, rs, mv, scale, eps):
                wait_apart(gp, mv_done[k], T * (batch + 1), gp_steps)
                gp.tensor_scalar(ve[:], mv[:, :, 1], scale, eps, ALU.mult, ALU.add).then_inc(ve_done[k], 1)
                wait(gp, ve_done[k], batch + 1)
                gp.tensor_tensor(rs[:], ve[:], minus_half[:, 0:T], ALU.pow).then_inc(rs_done[k], 1)

            def rstd_first(nb):
                rstd(0, nb, ve1, rs1, mv1, 1.0 + EPS_RMS, EPS_LN * EPS_RMS)

            def rstd_post(k, p):
                rstd(k, p, ln[k - 1][2], ln[k - 1][3], ln[k - 1][1], 1.0, EPS_LN)

            def squares(nb, t):
                n = T * nb + t
                wait(gp, pj_copied, PJ * n + 3)
                wait(gp, ssq_done, n)
                gp.tensor_tensor(sq[:], raw[t % 2][:], raw[t % 2][:], ALU.mult).then_inc(sq_done, 1)

            def norms(nb, t):
                n = T * nb + t
                wait(gp, ssq_done, n + 1)
                wait_apart(gp, rn_done, n, gp_steps)
                gp.tensor_scalar(ssg[:], ssq[t % 2][:], 1e-24, None, ALU.max).then_inc(ssg_done, 1)
                wait(gp, ssg_done, n + 1)
                wait(gp, qn_done, 3 * (n - 1))
                gp.tensor_tensor(rn[t % 2][:], ssg[:], minus_half[:], ALU.pow).then_inc(rn_done, 1)

            def mask(b, h):
                q = KH * b + h
                wait_apart(gp, exp_done, q + 1, gp_steps)
                pr = prob[h % 2]
                blocks = (pr[:, 0:1024].rearrange("p (g n) -> p g n", g=G)[:, :, 0:P],
                          pr[:, 1024:2560].rearrange("p (j g n) -> p j g n", j=2, g=G)[:, :, :, 0:P],
                          pr[:, 1792:2560].rearrange("p (g n) -> p g n", g=G)[:, :, 256:256 + P])
                for k, blk in enumerate(blocks):
                    gp.affine_select(out=blk, in_=blk, compare_op=ALU.is_ge, fill=0.0, base=0,
                                     pattern=[[0, 2], [0, 2], [1, P]] if k == 1 else [[0, 2], [1, P]],
                                     channel_multiplier=-1).then_inc(mask_done, 1)

            def iteration(b, par, prep, post):
                for h in range(KH):
                    if h == 0 and prep:
                        rstd_first(b + 1)
                    if prep and 3 <= h <= 6:
                        norms(b + 1, h - 3)
                    if prep and 2 <= h <= 5:
                        squares(b + 1, h - 2)
                    if post and h in (2, 3, 5):
                        rstd_post({2: 1, 3: 2, 5: 3}[h], b - 1)
                    mask(b, h)

            rstd_first(0)
            squares(0, 0)
            for t in range(T):
                norms(0, t)
                if t + 1 < T:
                    squares(0, t + 1)
            batches(gp, iteration)
            for k in (1, 2, 3):
                rstd_post(k, B - 1)

        @block.vector
        def _(ve):
            def setup():
                ve.wait_ge(s_g, 48)
                ve.tensor_scalar(gk8p[:], gk8[:], 1.0, None, ALU.add).then_inc(s_setup, 1)
                ve.wait_ge(s_setup, 1)
                ve.scalar_tensor_tensor(out=g8[:].rearrange("p (g d) -> p g d", g=G), in0=gq8[:], scalar=1.0,
                                        in1=gk8p[:], op0=ALU.add, op1=ALU.mult).then_inc(s_setup, 1)
                ve.wait_ge(s_w, 48)
                ve.tensor_scalar(w_all[:], w_all[:], nw_col[:, 0:1], None, ALU.mult).then_inc(s_setup, 1)
                ve.wait_ge(s_pe0, 1)
                ve.tensor_copy(gain[:], bank[0][:, 0:KH]).then_inc(s_setup, 1)
                ve.wait_ge(s_pe0, 2)
                ve.tensor_copy(a_t[:, 0, :], bank[1][:, 0:P]).then_inc(s_setup, 1)
                ve.tensor_copy(a_t[:, 1, :], bank[1][:, P:2 * P]).then_inc(s_setup, 1)
                ve.wait_ge(s_pe0, 3)
                ve.tensor_copy(bias_all[:], bank[0][:, 0:P]).then_inc(s_setup, 1)
                ve.wait_ge(s_pe0, 4)
                ve.tensor_scalar(mix[:], bank[1][:, 0:P], 1.0 / D, None, ALU.mult).then_inc(s_setup, 1)

            def stats(k, batch, src, st, mv):
                for t in range(T):
                    ve.bn_stats(st[:, t, :], src[:, t, :]).then_inc(st_done[k], 1)
                for t in range(T):
                    wait_apart(ve, st_done[k], T * batch + t + 1, ve_steps)
                    ve.bn_aggr(mv[:, t, :], st[:, t, :]).then_inc(mv_done[k], 1)

            def apply(dst, src, mv, rs, done):
                for t in range(T):
                    ve.tensor_scalar(dst[:, t, :], src[:, t, :], mv[:, t, 0:1], rs[:, t:t + 1],
                                     ALU.subtract, ALU.mult).then_inc(done, 1)

            def stats_first(nb, npar):
                wait(ve, x_loaded[npar], 8 * nb + 16 - 8 * npar)
                wait(ve, xn_done, T * nb)
                stats(0, nb, xin[npar], st1, mv1)

            def norm_first(nb, npar):
                wait(ve, rs_done[0], nb + 1)
                wait(ve, xt_done, nb)
                apply(xn, xin[npar], mv1, rs1, xn_done)

            def sum_squares(nb, t):
                n = T * nb + t
                wait(ve, sq_done, n + 1)
                wait(ve, ssg_done, n - 1)
                ve.tensor_reduce(ssq[t % 2][:], sq[:].rearrange("p (h d) -> p h d", d=DH), AX.X, ALU.add)\
                  .then_inc(ssq_done, 1)

            def norm_qk(nb, t):
                n = T * nb + t
                wait(ve, rn_done, n + 1)
                wait(ve, tr_done, TR * (n - 1))
                nq = QW // DH
                r = rn[t % 2][:].rearrange("p (h o) -> p h o", o=1)
                ve.tensor_tensor(qn[t % 2][:, 0:QW].rearrange("p (h d) -> p h d", d=DH),
                                 raw[t % 2][:, 0:QW].rearrange("p (h d) -> p h d", d=DH),
                                 r[:, 0:nq].broadcast_to([P, nq, DH]), ALU.mult).then_inc(qn_done, 1)
                for k in range(2):
                    ve.tensor_tensor(qn[t % 2][:, QW:].rearrange("p (h k d) -> p h k d", k=2, d=DH)[:, :, k],
                                     raw[t % 2][:, QW:].rearrange("p (h d) -> p h d", d=DH),
                                     r[:, nq:].broadcast_to([P, KH, DH]), ALU.mult).then_inc(qn_done, 1)

            def q_copy(nb, npar, t):
                n = T * nb + t
                for c in range(2):
                    wait(ve, tr_done, TR * n + c + 1)
                    if c == 0:
                        wait(ve, s_done, 24 * (nb - 1))
                    h = 4 * c
                    ve.tensor_tensor(qT[npar][:, h:h + 4, t * P:(t + 1) * P],
                                     bank[c][:].rearrange("p (h n) -> p h n", n=P),
                                     gain[:, h:h + 4].rearrange("p (h o) -> p h o", o=1)
                                     .broadcast_to([P, 4, P]), ALU.mult).then_inc(qT_ready, 1)

            def weigh(b, par, h):
                q = KH * b + h
                wait(ve, av_done, q + 1)
                wait(ve, og_done, q)
                ve.reciprocal(rden[:], acc_o[:, :, :, DH]).then_inc(rden_done, 1)
                wait(ve, rden_done, q + 1)
                wait(ve, o_done, q)
                ve.tensor_tensor(og[:], acc_o[:, :, :, 0:DH],
                                 rden[:].rearrange("p g (t o) -> p g t o", o=1).broadcast_to([P, G, T, DH]),
                                 ALU.mult).then_inc(og_done, 1)
                wait(ve, og_done, q + 1)
                ve.tensor_tensor(otok[par][:, :, h * DH:(h + 1) * DH], og[:, 0], og[:, 1], ALU.add)\
                  .then_inc(o_done, 1)

            def o_copy(p):
                for t in range(T):
                    wait(ve, ot_done, T * p + t + 1)
                    ve.tensor_copy(oT[:, t].rearrange("p c n -> p (c n)"), bank[1 - t % 2][:])\
                      .then_inc(ot_copied, 1)

            def attn_stats(p):
                wait(ve, op_copied, p + 1)
                stats(1, p, attn, ln[0][0], ln[0][1])

            def first_residual(p):
                wait(ve, rs_done[1], p + 1)
                apply(z2, attn, ln[0][1], ln[0][3], z2_done)
                wait(ve, z2_done, T * (p + 1))
                wait(ve, r_loaded, 16 * (p + 1))
                ve.tensor_tensor(x1[:], z2[:], xres[:], ALU.add).then_inc(x1_done, 1)
                wait(ve, x1_done, p + 1)
                stats(2, p, x1, ln[1][0], ln[1][1])

            def mix_norm(p):
                wait(ve, rs_done[2], p + 1)
                apply(xn3, x1, ln[1][1], ln[1][3], xn3_done)

            def mix_out(p):
                wait(ve, ff_done, p + 1)
                ve.tensor_tensor(y[:], bank[1][:].rearrange("p (t d) -> p t d", d=D),
                                 bias_all[:].rearrange("p (o d) -> p o d", o=1).broadcast_to([P, T, D]),
                                 ALU.add).then_inc(y_done, 1)
                wait(ve, y_done, p + 1)
                stats(3, p, y, ln[2][0], ln[2][1])

            def second_residual(p):
                wait(ve, rs_done[3], p + 1)
                apply(z4, y, ln[2][1], ln[2][3], z4_done)
                wait(ve, z4_done, T * (p + 1))
                wait(ve, res_free, 16 * (p + 1))
                ve.tensor_tensor(res[:], z4[:], x1[:], ALU.add).then_inc(res_done, 1)
                wait(ve, res_done, p + 1)

            def iteration(b, par, prep, post):
                for h in range(KH):
                    if h >= 2:
                        weigh(b, par, h - 2)
                    elif post:
                        weigh(b - 1, 1 - par, KH - 2 + h)
                    if prep and h == 0:
                        stats_first(b + 1, 1 - par)
                        norm_first(b + 1, 1 - par)
                    if post and h == 1:
                        o_copy(b - 1)
                    if post and h == 2:
                        attn_stats(b - 1)
                    if prep and 3 <= h <= 6:
                        sum_squares(b + 1, h - 3)
                    if post and h == 3:
                        first_residual(b - 1)
                    if post and h == 4:
                        mix_norm(b - 1)
                    if post and h == 5:
                        mix_out(b - 1)
                    if prep and h >= 4:
                        q_copy(b + 1, 1 - par, h - 4)
                    if prep and 3 <= h <= 6:
                        norm_qk(b + 1, h - 3)
                    if post and h == 6:
                        second_residual(b - 1)

            ve.wait_ge(s_const, 5)
            stats_first(0, 0)
            setup()
            norm_first(0, 0)
            sum_squares(0, 0)
            norm_qk(0, 0)
            sum_squares(0, 1)
            q_copy(0, 0, 0)
            norm_qk(0, 1)
            for t in (2, 3):
                sum_squares(0, t)
                q_copy(0, 0, t - 1)
                norm_qk(0, t)
            q_copy(0, 0, 3)
            batches(ve, iteration)
            weigh(B - 1, (B - 1) % 2, KH - 2)
            weigh(B - 1, (B - 1) % 2, KH - 1)
            o_copy(B - 1)
            attn_stats(B - 1)
            first_residual(B - 1)
            mix_norm(B - 1)
            mix_out(B - 1)
            second_residual(B - 1)


_INS = ["L0_attn_tokens", "L0_attn_norm_w", "L0_attn_Wq", "L0_attn_Wkv", "L0_attn_Wout",
        "L0_attn_q_gamma", "L0_attn_k_gamma", "L0_ffn_w_freq_real", "L0_ffn_w_freq_imag", "L0_ffn_bias"]


def kernel(**inputs):
    import numpy as _np
    import concourse.bacc as _bacc
    from concourse import mybir as _mybir
    from concourse.bass_utils import run_bass_kernel_spmd as _run

    nc = _bacc.Bacc("TRN2", target_bir_lowering=False, num_devices=1)
    arrays, args = {}, []
    for name in _INS:
        a = _np.ascontiguousarray(inputs[name])
        arrays[f"in_{name}_dram"] = a
        args.append(nc.dram_tensor(f"in_{name}_dram", a.shape, _mybir.dt.from_np(a.dtype), kind="ExternalInput").ap())
    angle = 2 * _np.pi / 128 * (_np.outer(_np.arange(128), _np.arange(128)) % 128)
    table = _np.stack([_np.cos(angle), _np.sin(angle), -_np.sin(angle)]).astype(_np.float32)
    arrays["dft_dram"] = table
    args.append(nc.dram_tensor("dft_dram", table.shape, _mybir.dt.float32, kind="ExternalInput").ap())
    o = nc.dram_tensor("out_0_dram", (8, 512, 128), _mybir.dt.float32, kind="ExternalOutput").ap()
    build(nc, *args, o)
    r = _run(nc, [arrays], core_ids=[0])
    return r.results[0]["out_0_dram"]
```

```python
import concourse.bass as bass
from concourse import mybir
from contextlib import ExitStack

FP32 = mybir.dt.float32
FP16 = mybir.dt.float16
INT32 = mybir.dt.int32
ALU = mybir.AluOpType
ACT = mybir.ActivationFunctionType
AX = mybir.AxisListType

P = 128
B, N, D = 8, 512, 128
KH, G, DH = 8, 2, 64
T = N // P
QW, KW = KH * G * DH, KH * DH
X_SCALE, W_SCALE = 64.0, 1024.0
V_SCALE = X_SCALE
EXP_BIAS = 4.5
QK_SCALE = 256.0
EPS_LN, EPS_RMS = 1e-5, 1.1920928955078125e-07
SOFTCLAMP = 50.0
UNITS = 3
P_AT = [[0, 512], [1024, 1408], [1792, 2176], [2048, 2432]]
P_LEN = 2560
P_DVE = 1536
RN_STEPS = 3 + 3 * 3
PJ, TR = 4, 4


def wait(eng, sem, value):
    if isinstance(value, int) and value <= 0:
        return
    eng.wait_ge(sem, value)


def wait_apart(eng, sem, value, steps):
    wait(eng, sem, value)
    if not isinstance(value, int):
        eng.sem_inc(steps, 1)


def min_batch(n):
    return min(n, B) if isinstance(n, int) else n


def build(nc, x, norm_w, wq, wkv, wout, q_gamma, k_gamma, w_real, w_imag, bias, dft, out):
    x_t = x.rearrange("b (t p) d -> b p t d", p=P)
    out_t = out.rearrange("b (t p) d -> b p t d", p=P)
    ctx = ExitStack()
    with ctx:
        def sb(name, shape, dtype=FP32):
            return ctx.enter_context(nc.sbuf_tensor(name, shape, dtype))

        def sem(name):
            return ctx.enter_context(nc.semaphore(name))

        w_hi = sb("w_hi", [P, QW + 2 * KW], FP16)
        w_lo = sb("w_lo", [P, QW + 2 * KW], FP16)
        w_top = sb("w_top", [P, 1]); w_max = sb("w_max", [1, 1]); w_guard = sb("w_guard", [1, 1])
        w_big = sb("w_big", [P, 1])
        w_unit = sb("w_unit", [P, 1]); w_unit2 = sb("w_unit2", [P, 1])
        norm_floor = sb("norm_floor", [P, 1])
        exp_bias = sb("exp_bias", [P, 1])
        w_out = sb("w_out", [P, 4, D])
        nw_col = sb("nw_col", [P, 1])
        mix = sb("mix", [P, P])
        bias_all = sb("bias_all", [P, P])
        ones_row = sb("ones_row", [1, P])
        ident = sb("ident", [P, P])
        ident16 = sb("ident16", [P, P], FP16)
        ones8 = sb("ones8", [KH, P])
        g8m = sb("g8m", [KH, 1]); g8g = sb("g8g", [KH, 1]); g8r = sb("g8r", [KH, 1])
        m8b = sb("m8b", [KH, KH])
        gain = sb("gain", [P, QW])
        clamp = sb("clamp", [P, KH])
        minus_half = sb("minus_half", [P, T])
        xin = [sb(f"xin{i}", [P, T, D]) for i in range(2)]
        xn = sb("xn", [P, T, D])
        xT_hi = sb("xT_hi", [P, T * P], FP16)
        xT_lo = sb("xT_lo", [P, T * P], FP16)
        st1 = sb("st1", [P, T, 6]); mv1 = sb("mv1", [P, T, 2]); ve1 = sb("ve1", [P, T]); rs1 = sb("rs1", [P, T])
        raw = [sb(f"raw{i}", [P, QW + KW]) for i in range(2)]
        sq = sb("sq", [P, QW])
        sqk = [sb(f"sqk{i}", [P, KW]) for i in range(2)]
        ssq = sb("ssq", [P, 2, 24])
        ssg = sb("ssg", [P, 48]); ssh = sb("ssh", [P, 48]); ysq = sb("ysq", [P, 48]); yxx = sb("yxx", [P, 48])
        bits = sb("bits", [P, 48], INT32)
        rn = sb("rn", [P, 2, 24])
        qn = sb("qn", [P, QW])
        kn = sb("kn", [P, KW])
        qs = [sb(f"qs{i}", [P, KH * G, 2, DH], FP16) for i in range(2)]
        ks = [sb(f"ks{i}", [P, KH, 3, DH], FP16) for i in range(2)]
        qT = [sb(f"qT{i}", [P, KH * G, N], FP16) for i in range(2)]
        kT = [sb(f"kT{i}", [P, KH * 2, N], FP16) for i in range(2)]
        vf = [sb(f"vf{i}", [P, KH, DH]) for i in range(2)]
        vs = [sb(f"vs{i}", [P, T, KH, 2 * DH + 2], FP16) for i in range(2)]
        prob = [sb(f"prob{i}", [P, P_LEN]) for i in range(2)]
        p_hi = sb("p_hi", [P, P_LEN], FP16)
        p_lo = sb("p_lo", [P, P_LEN], FP16)
        small = [sq[0:KH, k * P:(k + 1) * P] for k in range(6)]
        gq8, gk8, gk8p = (a.rearrange("p (g d) -> p g d", g=G) for a in small[:3])
        g8, g8a, g8n = small[3:]
        g8b = qn[0:KH, :].rearrange("p (h d) -> p h d", h=KH)
        tables = raw[1][:, 0:3 * P].rearrange("p (k n) -> p k n", k=3)
        wf = raw[1][:, 3 * P:5 * P].rearrange("p (k n) -> p k n", k=2)
        a_t = raw[1][:, 5 * P:7 * P].rearrange("p (k n) -> p k n", k=2)
        bias_row = raw[1][0:1, 7 * P:8 * P]
        w_all = prob[0][:, 0:QW + 2 * KW]
        w_abs = prob[1][:, 0:QW + 2 * KW]
        rden = sb("rden", [P, G, T])
        og = sb("og", [P, G, T, DH])
        otok = sb("otok", [P, T, KW])
        oT = sb("oT", [P, T, 4, P])
        attn = sb("attn", [P, T, D])
        xres = sb("xres", [P, T, D])
        z2 = sb("z2", [P, T, D])
        x1 = xres
        xn3 = z2
        x3T = sb("x3T", [P, T * P])
        y = attn
        z4 = z2
        res = z2
        ln = [[sb(f"ln{k}_{i}", [P, T, w] if w > 1 else [P, T]) for i, w in enumerate((6, 2, 1, 1))]
              for k in range(3)]

        score = [ctx.enter_context(nc.psum_tensor(f"score{i}", [P, 2, 512], FP32)) for i in range(2)]
        acc = ctx.enter_context(nc.psum_tensor("acc", [P, G, 512], FP32))
        bank = [ctx.enter_context(nc.psum_tensor(f"bank{i}", [P, 512], FP32)) for i in range(2)]
        bank16 = [bk[:].bitcast(FP16) for bk in bank]
        acc_o = acc[:, :, 0:T * (DH + 1)].rearrange("p g (t c) -> p g t c", c=DH + 1)

        s_const = sem("s_const"); s_setup = sem("s_setup"); s_gp = sem("s_gp"); s_pe0 = sem("s_pe0")
        s_w = sem("s_w"); s_tab = sem("s_tab"); s_g = sem("s_g"); s_g8 = sem("s_g8"); s_wabs = sem("s_wabs"); s_wout = sem("s_wout")
        ve_steps = sem("ve_steps"); gp_steps = sem("gp_steps")
        x_loaded = [sem("x_even_loaded"), sem("x_odd_loaded")]; r_loaded = sem("r_loaded"); res_free = sem("res_free")
        st_done = [sem(f"st{k}_done") for k in range(4)]
        mv_done = [sem(f"mv{k}_done") for k in range(4)]
        ve_done = [sem(f"ve{k}_done") for k in range(4)]
        rs_done = [sem(f"rs{k}_done") for k in range(4)]
        xn_done = sem("xn_done"); xt_done = sem("xt_done"); xt_copied = sem("xt_copied")
        pj_done = sem("pj_done"); pj_copied = sem("pj_copied")
        vhi_done = sem("vhi_done"); sq_done = sem("sq_done"); sqk_done = sem("sqk_done"); ssq_done = sem("ssq_done"); rn_chain = sem("rn_chain")
        qn_done = sem("qn_done"); qg_done = sem("qg_done")
        xlo_copied = sem("xlo_copied"); vlo_done = sem("vlo_done")
        phi_done = sem("phi_done"); plo_done = sem("plo_done"); s_wn = sem("s_wn"); s_wp = sem("s_wp")
        hi_done = sem("hi_done"); lo_done = sem("lo_done")
        tr_done = sem("tr_done"); tr_copied = sem("tr_copied")
        s_done = sem("s_done"); tanh_done = sem("tanh_done"); exp_done = sem("exp_done")
        mask_done = sem("mask_done"); av_done = sem("av_done")
        rden_done = sem("rden_done"); og_done = sem("og_done"); o_done = sem("o_done")
        ot_done = sem("ot_done"); ot_copied = sem("ot_copied"); op_done = sem("op_done")
        op_copied = sem("op_copied"); z2_done = sem("z2_done"); x1_done = sem("x1_done")
        xn3_done = sem("xn3_done"); ft_done = sem("ft_done"); ft_copied = sem("ft_copied")
        ff_done = sem("ff_done"); y_done = sem("y_done"); z4_done = sem("z4_done")
        res_done = sem("res_done")

        block = ctx.enter_context(nc.Block())

        def batches(eng, iteration):
            iteration(0, 0, True, False, True)
            with eng.Fori(1, B - 3, 2) as b:
                iteration(b, 1, True, True, True)
                iteration(b + 1, 0, True, True, True)
            iteration(B - 3, 1, True, True, True)
            iteration(B - 2, 0, True, True, False)
            iteration(B - 1, 1, False, True, False)

        @block.sync
        def _(sp):
            sp.sem_inc(res_free, 16)
            sp.dma_start(xin[0][:], x_t[0]).then_inc(x_loaded[0], 16)
            sp.dma_start(prob[0][:, 0:QW], wq).then_inc(s_w, 16)
            sp.dma_start(prob[0][:, QW:QW + 2 * KW], wkv).then_inc(s_w, 16)
            sp.dma_start(nw_col[:], norm_w.rearrange("(d o) -> d o", o=1)).then_inc(s_w, 16)
            sp.dma_start(xin[1][:], x_t[1]).then_inc(x_loaded[1], 16)
            sp.dma_start(gq8, q_gamma.rearrange("(h g) d -> h g d", g=G)).then_inc(s_g, 16)
            for g in range(G):
                sp.dma_start(gk8[:, g, :], k_gamma).then_inc(s_g, 16)
            sp.dma_start(w_out[:], wout.rearrange("(c p) d -> p c d", p=P)).then_inc(s_tab, 16)
            sp.dma_start(tables, dft.rearrange("k p d -> p k d")).then_inc(s_tab, 16)
            sp.dma_start(wf[:, 0, :], w_real).then_inc(s_tab, 16)
            sp.dma_start(wf[:, 1, :], w_imag).then_inc(s_tab, 16)
            sp.dma_start(bias_row, bias.rearrange("(o d) -> o d", o=1)).then_inc(s_tab, 16)

            def load_next(b, par):
                wait(sp, xn_done, T * (b + 1))
                sp.dma_start(xin[par][:], x_t[b + 2]).then_inc(x_loaded[par], 16)

            def load_residual(b):
                wait(sp, res_done, b)
                sp.dma_start(xres[:], x_t[b]).then_inc(r_loaded, 16)

            def store(p):
                wait(sp, res_done, p + 1)
                sp.dma_start(out_t[p], res[:]).then_inc(res_free, 16)

            def iteration(b, par, prep):
                if prep:
                    load_next(b, par)
                load_residual(b)
                if not (isinstance(b, int) and b == 0):
                    store(b - 1)

            iteration(0, 0, True)
            with sp.Fori(1, B - 3, 2) as b:
                iteration(b, 1, True)
                iteration(b + 1, 0, True)
            iteration(B - 3, 1, True)
            iteration(B - 2, 0, False)
            iteration(B - 1, 1, False)
            store(B - 1)
            sp.wait_ge(res_free, 16 * (B + 1))

        @block.tensor
        def _(pe):
            def setup():
                pe.wait_ge(s_const, 8)
                pe.wait_ge(s_g8, 8)
                for c in range(2):
                    mm = pe.matmul(score[0][:, c, :], ones8[:], g8b[:, 4 * c:4 * c + 4, :].rearrange("p h d -> p (h d)"),
                                   start=True, stop=True)
                pe.matmul(bank[0][:, 0:KH], ones8[:], m8b[:], start=True, stop=True).then_inc(s_pe0, 1)
                pe.wait_ge(s_wn, 2)
                pe.transpose(score[1][0:1, 0, 0:P], w_top[:], ident[:]).then_inc(s_wp, 1)
                pe.wait_ge(s_wn, 4)
                pe.matmul(score[1][:, 1, 0:1], ones_row[:], w_guard[:], start=True, stop=True).then_inc(s_wp, 1)
                pe.wait_ge(s_tab, 80)
                cos, sin, msin = (tables[:, k, :] for k in range(3))
                wr, wi = wf[:, 0, :], wf[:, 1, :]
                pe.matmul(bank[1][:, 0:P], wr, cos, start=True, stop=False)
                pe.matmul(bank[1][:, 0:P], wi, sin, start=False, stop=True)
                pe.matmul(bank[1][:, P:2 * P], wi, cos, start=True, stop=False)
                pe.matmul(bank[1][:, P:2 * P], wr, msin, start=False, stop=True).then_inc(s_pe0, 1)
                pe.wait_ge(s_setup, 4)
                pe.matmul(bank[0][:, 0:P], ones_row[:], bias_row, start=True, stop=True).then_inc(s_pe0, 1)
                pe.wait_ge(s_setup, 6)
                pe.matmul(bank[1][:, 0:P], a_t[:, 0, :], cos, start=True, stop=False)
                pe.matmul(bank[1][:, 0:P], a_t[:, 1, :], msin, start=False, stop=True).then_inc(s_pe0, 1)

            def x_transpose(nb):
                wait(pe, tr_copied, TR * T * nb - 1)
                wait(pe, xn_done, T * (nb + 1))
                for t in range(T):
                    mm = pe.transpose(bank[0][:, t * P:(t + 1) * P], xn[:, t, :], ident[:])
                mm.then_inc(xt_done, 1)

            def project(nb, t, post, half):
                n, p = T * nb + t, nb - 2
                if t == 0:
                    wait(pe, xt_copied, nb + 1)
                    wait(pe, xlo_copied, nb + 1)
                for c in (2 * half, 2 * half + 1):
                    if c >= 2:
                        wait(pe, pj_copied, PJ * n + c - 1)
                    elif t == 0:
                        wait(pe, tr_copied, 16 * nb)
                    elif post and t == 2:
                        wait(pe, ot_copied, T * p + 3 + c)
                    elif post and t == 3 and c == 0:
                        wait(pe, op_copied, p + 1)
                    else:
                        wait(pe, pj_copied, PJ * n - 1 + c)
                    tile, cols = slice(t * P, (t + 1) * P), slice(c * 512, (c + 1) * 512)
                    pe.matmul(bank[c % 2][:], xT_hi[:, tile], w_hi[:, cols], start=True, stop=False)
                    pe.matmul(bank[c % 2][:], xT_hi[:, tile], w_lo[:, cols], start=False, stop=False)
                    pe.matmul(bank[c % 2][:], xT_lo[:, tile], w_hi[:, cols], start=False, stop=False)
                    pe.matmul(bank[c % 2][:], xT_lo[:, tile], w_lo[:, cols], start=False, stop=True)\
                      .then_inc(pj_done, 1)

            def transposes(nb, t, post, half):
                n, p = T * nb + t, nb - 2
                wait(pe, lo_done, 2 * (n + 1))
                for c in (2 * half, 2 * half + 1):
                    if c >= 2:
                        wait(pe, tr_copied, TR * n + c - 1)
                    elif t == 0:
                        wait(pe, pj_copied, PJ * (n + 3) + 3 + c)
                    elif post and t == 2:
                        wait(pe, *((ft_copied, p + 1), (y_done, p + 1))[c])
                    else:
                        wait(pe, tr_copied, TR * n - 1 + c)
                    for k in range(8):
                        h, half = 4 * (c - 2) + k // 2, k % 2
                        src = qs[t % 2][:, 8 * c + k] if c < 2 else ks[t % 2][:, h, half:half + 2]
                        mm = pe.transpose(bank16[c % 2][:, k * P:(k + 1) * P],
                                          src.rearrange("p s d -> p (s d)"), ident16[:])
                    mm.then_inc(tr_done, 1)

            def scores(b, par, h, u):
                q = KH * b + h
                if h == 0 and u == 0:
                    wait(pe, tr_copied, 16 * (b + 1))
                wait(pe, tanh_done, UNITS * q + u - 1)
                s = score[(UNITS * h + u) % 2]
                for j, at in (((0, 0),), ((1, 0),), ((2, 0), (3, 256)))[u]:
                    for half in range(2):
                        for g in range(G):
                            mm = pe.matmul(s[:, g, at:at + N - j * P], kT[par][:, 2 * h + half, j * P:(j + 1) * P],
                                           qT[par][:, G * h + g, j * P:N], start=(half == 0), stop=(half == 1))
                mm.then_inc(s_done, 1)

            def values(b, par, h, g):
                q = KH * b + h
                if g == 0:
                    if h == 0:
                        wait(pe, vhi_done, T * (b + 1))
                        wait(pe, vlo_done, T * (b + 1))
                    wait(pe, og_done, q)
                    wait(pe, plo_done, 2 * (q + 1))
                for t in range(T):
                    o = acc[:, g, t * (DH + 1):(t + 1) * (DH + 1)]
                    for j in range(t + 1):
                        at = P_AT[j][g] + (t - j) * P
                        for k, pr in enumerate((p_hi, p_lo)):
                            pe.matmul(o, pr[:, at:at + P], vs[par][:, j, h, 0:DH + 1],
                                      start=(j == 0 and k == 0), stop=False)
                            mm = pe.matmul(o[:, 0:DH], pr[:, at:at + P], vs[par][:, j, h, DH + 2:],
                                           start=False, stop=(j == t and k == 1))
                if g == G - 1:
                    mm.then_inc(av_done, 1)

            def o_transposes(p, prep, half):
                if half == 0:
                    wait(pe, o_done, KH * (p + 1))
                for t in (2 * half, 2 * half + 1):
                    if half == 1:
                        wait(pe, ot_copied, T * p + t - 1)
                    elif prep:
                        wait(pe, pj_copied, PJ * (T * (p + 2) + 1) + 3 + t)
                    for c in range(4):
                        mm = pe.transpose(bank[t % 2][:, c * P:(c + 1) * P],
                                          otok[:, t, c * P:(c + 1) * P], ident[:])
                    mm.then_inc(ot_done, 1)

            def out_project(p, prep):
                if isinstance(p, int) and p == 0:
                    pe.wait_ge(s_wout, 1)
                if prep:
                    wait(pe, pj_copied, PJ * (T * (p + 2) + 2) + 3)
                wait(pe, ot_copied, T * (p + 1))
                for t in range(T):
                    for c in range(4):
                        mm = pe.matmul(bank[0][:, t * P:(t + 1) * P], oT[:, t, c, :], w_out[:, c, :],
                                       start=(c == 0), stop=(c == 3))
                mm.then_inc(op_done, 1)

            def f_transpose(p, prep):
                wait(pe, xn3_done, T * (p + 1))
                if prep:
                    wait(pe, tr_copied, TR * (T * (p + 2) + 1) + 3)
                for t in range(T):
                    mm = pe.transpose(bank[0][:, t * P:(t + 1) * P], xn3[:, t, :], ident[:])
                mm.then_inc(ft_done, 1)

            def f_mix(p, prep):
                wait(pe, ft_copied, p + 1)
                if prep:
                    wait(pe, tr_copied, TR * (T * (p + 2) + 1) + 4)
                for t in range(T):
                    mm = pe.matmul(bank[1][:, t * P:(t + 1) * P], x3T[:, t * P:(t + 1) * P], mix[:],
                                   start=True, stop=True)
                mm.then_inc(ff_done, 1)

            def extra(b, h, place, prep, post, ahead):
                nb, p = b + 1, b - 1
                if ahead and (h, place) == (7, 2):
                    x_transpose(b + 2)
                if prep and h == 0 and place >= 2:
                    project(nb, 0, post, place - 2)
                if prep and h in (1, 2, 3) and place < 2:
                    project(nb, h, post, place)
                if post and h == 1 and place >= 2:
                    o_transposes(p, prep, place - 2)
                if post and (h, place) == (2, 2):
                    out_project(p, prep)
                if prep and h in (3, 4) and place >= 2:
                    transposes(nb, h - 3, post, place - 2)
                if post and (h, place) == (5, 2):
                    f_transpose(p, prep)
                if post and (h, place) == (5, 3):
                    f_mix(p, prep)
                if prep and h == 6 and place in (1, 2):
                    transposes(nb, 2, post, place - 1)
                if prep and h == 7 and place < 2:
                    transposes(nb, 3, post, place)

            def iteration(b, par, prep, post, ahead):
                for h in range(KH):
                    for u in range(UNITS):
                        scores(b, par, h, u)
                        extra(b, h, u, prep, post, ahead)
                    for g in range(G):
                        if h >= 1:
                            values(b, par, h - 1, g)
                        elif post:
                            values(b - 1, 1 - par, KH - 1, g)
                        if g == 0:
                            extra(b, h, 3, prep, post, ahead)

            setup()
            pe.wait_ge(s_setup, 8)
            x_transpose(0)
            for t in range(T):
                for half in range(2):
                    project(0, t, False, half)
            for t in range(T):
                for half in range(2):
                    transposes(0, t, False, half)
            x_transpose(1)
            batches(pe, iteration)
            for g in range(G):
                values(B - 1, (B - 1) % 2, KH - 1, g)
            for half in range(2):
                o_transposes(B - 1, False, half)
            out_project(B - 1, False)
            f_transpose(B - 1, False)
            f_mix(B - 1, False)

        @block.scalar
        def _(act):
            def x_copy(nb):
                wait(act, xt_done, nb + 1)
                wait(act, pj_done, 16 * nb)
                act.activation(xT_hi[:], bank[0][:], ACT.Copy, scale=X_SCALE).then_inc(xt_copied, 1)

            def p_copy(nb, npar, t, half):
                n = T * nb + t
                for c in (2 * half, 2 * half + 1):
                    wait(act, pj_done, PJ * n + c + 1)
                    if c == 0:
                        wait(act, qn_done, 2 * (n - 1))
                    if c == 2:
                        wait(act, ssq_done, 2 * (n - 1))
                        act.activation(sqk[t % 2][:], bank[0][:], ACT.Square).then_inc(sqk_done, 1)
                    if c < 3:
                        act.copy(raw[t % 2][:, c * 512:(c + 1) * 512], bank[c % 2][:]).then_inc(pj_copied, 1)
                    else:
                        if t == 0:
                            wait(act, av_done, KH * (nb - 1))
                        act.activation(vs[npar][:, t, :, 0:DH], bank[1][:].rearrange("p (h d) -> p h d", d=DH),
                                       ACT.Copy, scale=1.0 / W_SCALE).then_inc(vhi_done, 1)
                        wait(act, vlo_done, n - 1)
                        act.activation(vf[t % 2][:].rearrange("p h d -> p (h d)"), bank[1][:],
                                       ACT.Copy, scale=1.0 / W_SCALE).then_inc(pj_copied, 1)

            def t_copy(nb, npar, t, half):
                n = T * nb + t
                for c in (2 * half, 2 * half + 1):
                    wait(act, tr_done, TR * n + c + 1)
                    if c in (0, 2):
                        wait(act, s_done, 24 * (nb - 1))
                    dst = (qT if c < 2 else kT)[npar]
                    h = 8 * (c % 2)
                    act.copy(dst[:, h:h + 8, t * P:(t + 1) * P],
                             bank16[c % 2].rearrange("p (h n) -> p h n", n=P)).then_inc(tr_copied, 1)

            def o_copy(p, half):
                for t in (2 * half, 2 * half + 1):
                    wait(act, ot_done, T * p + t + 1)
                    act.copy(oT[:, t].rearrange("p c n -> p (c n)"), bank[t % 2][:]).then_inc(ot_copied, 1)

            def tanh(b, h, u):
                q = KH * b + h
                if u == 0:
                    wait(act, plo_done, 2 * (q - 1))
                wait(act, s_done, UNITS * q + u + 1)
                w = 512 if u == 0 else 384
                at = P_AT[u][0]
                act.activation(prob[h % 2][:, at:at + 2 * w].rearrange("p (g n) -> p g n", g=G),
                               score[(UNITS * h + u) % 2][:, :, 0:w], ACT.Tanh,
                               scale=clamp[:, h:h + 1]).then_inc(tanh_done, 1)

            def exp(b, h):
                q = KH * b + h
                wait(act, tanh_done, UNITS * (q + 1))
                act.activation(prob[h % 2][:], prob[h % 2][:], ACT.Exp, bias=exp_bias[:, 0:1],
                               scale=SOFTCLAMP * DH ** -0.5).then_inc(exp_done, 1)

            def attn_copy(p):
                wait(act, op_done, p + 1)
                act.copy(attn[:].rearrange("p t d -> p (t d)"), bank[0][:]).then_inc(op_copied, 1)

            def f_copy(p):
                wait(act, ft_done, p + 1)
                act.copy(x3T[:], bank[0][:]).then_inc(ft_copied, 1)

            def extra(b, par, h, place, prep, post, ahead):
                nb, npar, p = b + 1, 1 - par, b - 1
                if ahead and (h, place) == (7, 2):
                    x_copy(b + 2)
                if prep and h == 0 and place >= 2:
                    p_copy(nb, npar, 0, place - 2)
                if prep and h in (1, 2, 3) and place < 2:
                    p_copy(nb, npar, h, place)
                if post and h == 1 and place >= 2:
                    o_copy(p, place - 2)
                if post and (h, place) == (2, 2):
                    attn_copy(p)
                if prep and h in (3, 4) and place >= 2:
                    t_copy(nb, npar, h - 3, place - 2)
                if post and (h, place) == (5, 2):
                    f_copy(p)
                if prep and h == 6 and place in (1, 2):
                    t_copy(nb, npar, 2, place - 1)
                if prep and h == 7 and place < 2:
                    t_copy(nb, npar, 3, place)

            def iteration(b, par, prep, post, ahead):
                for h in range(KH):
                    for u in range(UNITS):
                        tanh(b, h, u)
                        extra(b, par, h, u, prep, post, ahead)
                    exp(b, h)
                    extra(b, par, h, 3, prep, post, ahead)

            x_copy(0)
            for t in range(T):
                for half in range(2):
                    p_copy(0, 0, t, half)
            for t in range(T):
                for half in range(2):
                    t_copy(0, 0, t, half)
            x_copy(1)
            batches(act, iteration)
            for half in range(2):
                o_copy(B - 1, half)
            attn_copy(B - 1)
            f_copy(B - 1)

        @block.gpsimd
        def _(gp):
            gp.memset(ident[:], 0.0).then_inc(s_gp, 1)
            gp.wait_ge(s_gp, 1)
            gp.affine_select(out=ident[:], in_=ident[:], compare_op=ALU.not_equal, fill=1.0, base=0,
                             pattern=[[-1, P]], channel_multiplier=1).then_inc(s_const, 1)
            gp.memset(minus_half[:], -0.5).then_inc(s_const, 1)
            gp.memset(ones_row[:], 1.0).then_inc(s_const, 1)
            gp.memset(ones8[:], 1.0).then_inc(s_const, 1)
            gp.memset(exp_bias[:], EXP_BIAS).then_inc(s_const, 1)
            gp.memset(ident16[:], 0.0).then_inc(s_gp, 1)
            gp.wait_ge(s_gp, 2)
            gp.affine_select(out=ident16[:], in_=ident16[:], compare_op=ALU.not_equal, fill=1.0, base=0,
                             pattern=[[-1, P]], channel_multiplier=1).then_inc(s_const, 1)
            for i in range(2):
                gp.memset(vs[i][:, :, :, DH:DH + 2], 1.0).then_inc(s_const, 1)

            def rstd(k, batch, ve, rs, mv, scale, eps):
                wait_apart(gp, mv_done[k], T * (batch + 1), gp_steps)
                gp.tensor_scalar(ve[:], mv[:, :, 1], scale, eps, ALU.mult, ALU.add).then_inc(ve_done[k], 1)
                wait(gp, ve_done[k], batch + 1)
                gp.tensor_tensor(rs[:], ve[:], minus_half[:, 0:T], ALU.pow).then_inc(rs_done[k], 1)

            def rstd_first(nb):
                rstd(0, nb, ve1, rs1, mv1, 1.0 + EPS_RMS, EPS_LN * EPS_RMS)

            def rstd_post(k, p):
                rstd(k, p, ln[k - 1][2], ln[k - 1][3], ln[k - 1][1], 1.0, EPS_LN)

            def squares(nb, t):
                n = T * nb + t
                wait(gp, pj_copied, PJ * n + 2)
                wait(gp, ssq_done, 2 * n)
                gp.tensor_tensor(sq[:], raw[t % 2][:, 0:QW], raw[t % 2][:, 0:QW], ALU.mult).then_inc(sq_done, 1)

            def gains(nb, t):
                n = T * nb + t
                wait(gp, qn_done, 2 * n + 1)
                gp.tensor_tensor(qn[:], qn[:], gain[:], ALU.mult).then_inc(qg_done, 1)

            def v_low(nb, npar, t):
                n = T * nb + t
                wait(gp, pj_copied, PJ * n + 4)
                gp.tensor_tensor(vs[npar][:, t, :, DH + 2:], vf[t % 2][:], vs[npar][:, t, :, 0:DH],
                                 ALU.subtract).then_inc(vlo_done, 1)

            def mask(b, h):
                q = KH * b + h
                wait_apart(gp, exp_done, q + 1, gp_steps)
                pr = prob[h % 2]
                blocks = (pr[:, 0:1024].rearrange("p (g n) -> p g n", g=G)[:, :, 0:P],
                          pr[:, 1024:2560].rearrange("p (j g n) -> p j g n", j=2, g=G)[:, :, :, 0:P],
                          pr[:, 1792:2560].rearrange("p (g n) -> p g n", g=G)[:, :, 256:256 + P])
                for k, blk in enumerate(blocks):
                    gp.affine_select(out=blk, in_=blk, compare_op=ALU.is_ge, fill=0.0, base=0,
                                     pattern=[[0, 2], [0, 2], [1, P]] if k == 1 else [[0, 2], [1, P]],
                                     channel_multiplier=-1).then_inc(mask_done, 1)

            def p_low(b, h):
                q = KH * b + h
                wait(gp, phi_done, q + 1)
                gp.tensor_tensor(p_lo[:, P_DVE:], prob[h % 2][:, P_DVE:], p_hi[:, P_DVE:], ALU.subtract)\
                  .then_inc(plo_done, 1)

            def apply(dst, src, k, done):
                for t in range(T):
                    gp.tensor_scalar(dst[:, t, :], src[:, t, :], ln[k][1][:, t, 0:1], ln[k][3][:, t:t + 1],
                                     ALU.subtract, ALU.mult).then_inc(done, 1)

            def first_residual(p):
                wait_apart(gp, rs_done[1], p + 1, gp_steps)
                wait_apart(gp, res_free, 16 * (p + 1), gp_steps)
                apply(z2, attn, 0, z2_done)
                wait(gp, z2_done, T * (p + 1))
                wait(gp, r_loaded, 16 * (p + 1))
                gp.tensor_tensor(x1[:], z2[:], xres[:], ALU.add).then_inc(x1_done, 1)

            def mix_norm(p):
                wait_apart(gp, x1_done, p + 1, gp_steps)
                wait_apart(gp, rs_done[2], p + 1, gp_steps)
                apply(xn3, x1, 1, xn3_done)

            def second_residual(p):
                wait_apart(gp, rs_done[3], p + 1, gp_steps)
                apply(z4, y, 2, z4_done)
                wait(gp, z4_done, T * (p + 1))
                gp.tensor_tensor(res[:], res[:], x1[:], ALU.add).then_inc(res_done, 1)

            def iteration(b, par, prep, post, ahead):
                for h in range(KH):
                    if ahead and h == 7:
                        rstd_first(b + 2)
                    if post and h == 5:
                        rstd_post(2, b - 1)
                        mix_norm(b - 1)
                    if prep and h in (2, 3, 5, 6):
                        gains(b + 1, {2: 0, 3: 1, 5: 2, 6: 3}[h])
                    if h >= 1:
                        p_low(b, h - 1)
                    elif post:
                        p_low(b - 1, KH - 1)
                    if prep and h < T:
                        squares(b + 1, h)
                        v_low(b + 1, 1 - par, h)
                    if post and h == 3:
                        rstd_post(1, b - 1)
                    if post and h == 4:
                        first_residual(b - 1)
                    if post and h == 7:
                        rstd_post(3, b - 1)
                        second_residual(b - 1)
                    mask(b, h)

            rstd_first(0)
            for m in range(2):
                for t in (2 * m, 2 * m + 1):
                    squares(0, t)
                    v_low(0, 0, t)
                gp.wait_ge(s_setup, 3)
                for t in (2 * m, 2 * m + 1):
                    gains(0, t)
            rstd_first(1)
            batches(gp, iteration)
            p_low(B - 1, KH - 1)
            rstd_post(1, B - 1)
            first_residual(B - 1)
            rstd_post(2, B - 1)
            mix_norm(B - 1)
            rstd_post(3, B - 1)
            second_residual(B - 1)

        @block.vector
        def _(ve):
            def setup():
                ve.wait_ge(s_w, 48)
                ve.tensor_scalar(w_all, w_all, nw_col[:, 0:1], None, ALU.mult).then_inc(s_wn, 1)
                ve.wait_ge(s_wn, 1)
                ve.scalar_tensor_tensor(out=w_abs, in0=w_all, scalar=-1.0, in1=w_all, op0=ALU.mult,
                                        op1=ALU.max).then_inc(s_wabs, 1)
                ve.wait_ge(s_wabs, 1)
                ve.tensor_reduce(w_top[:], w_abs, AX.X, ALU.max).then_inc(s_wn, 1)
                ve.wait_ge(s_g, 48)
                ve.tensor_scalar(gk8p, gk8, 1.0, None, ALU.add).then_inc(s_g8, 1)
                ve.wait_ge(s_g8, 1)
                ve.scalar_tensor_tensor(out=g8.rearrange("p (g d) -> p g d", g=G), in0=gq8, scalar=1.0,
                                        in1=gk8p, op0=ALU.add, op1=ALU.mult).then_inc(s_g8, 1)
                ve.wait_ge(s_g8, 2)
                ve.scalar_tensor_tensor(out=g8a, in0=g8, scalar=-1.0, in1=g8, op0=ALU.mult,
                                        op1=ALU.max).then_inc(s_g8, 1)
                ve.wait_ge(s_g8, 3)
                ve.tensor_reduce(g8m[:], g8a, AX.X, ALU.max).then_inc(s_g8, 1)
                ve.wait_ge(s_g8, 4)
                ve.tensor_scalar(g8g[:], g8m[:], 1e-30, None, ALU.max).then_inc(s_g8, 1)
                ve.wait_ge(s_g8, 5)
                ve.reciprocal(g8r[:], g8g[:]).then_inc(s_g8, 1)
                ve.wait_ge(s_g8, 6)
                ve.tensor_scalar(g8n, g8, g8r[:, 0:1], None, ALU.mult).then_inc(s_g8, 1)
                ve.tensor_scalar(m8b[:], ident[0:KH, 0:KH], g8g[:, 0:1], DH / SOFTCLAMP / QK_SCALE ** 2,
                                 ALU.mult, ALU.mult)
                ve.wait_ge(s_g8, 7)
                ve.tensor_tensor(g8b, g8n.rearrange("p (o d) -> p o d", o=1).broadcast_to([KH, KH, P]),
                                 ident[0:KH, 0:KH].rearrange("p (h o) -> p h o", o=1)
                                 .broadcast_to([KH, KH, P]), ALU.mult).then_inc(s_g8, 1)
                ve.wait_ge(s_wp, 1)
                ve.tensor_reduce(w_max[:], score[1][0:1, 0, 0:P], AX.X, ALU.max).then_inc(s_wn, 1)
                ve.wait_ge(s_wn, 3)
                ve.tensor_scalar(w_guard[:], w_max[:], 1e-20, None, ALU.max).then_inc(s_wn, 1)
                ve.wait_ge(s_wp, 2)
                ve.tensor_copy(w_big[:], score[1][:, 1, 0:1]).then_inc(s_wn, 1)
                ve.wait_ge(s_wn, 5)
                ve.reciprocal(w_unit[:], w_big[:]).then_inc(s_wn, 1)
                ve.wait_ge(s_wn, 6)
                ve.tensor_scalar(w_all, w_all, w_unit[:, 0:1], W_SCALE, ALU.mult, ALU.mult).then_inc(s_wn, 1)
                ve.tensor_scalar(w_unit2[:], w_unit[:], 1e-12 * X_SCALE * W_SCALE, None, ALU.mult)\
                  .then_inc(s_wn, 1)
                ve.wait_ge(s_wn, 8)
                ve.tensor_tensor(norm_floor[:], w_unit2[:], w_unit2[:], ALU.mult).then_inc(s_setup, 1)
                ve.tensor_copy(w_hi[:], w_all).then_inc(s_wn, 1)
                ve.wait_ge(s_wn, 9)
                ve.tensor_tensor(w_lo[:], w_all, w_hi[:], ALU.subtract).then_inc(s_setup, 1)
                ve.wait_ge(s_tab, 80)
                ve.tensor_scalar(w_out[:], w_out[:], w_big[:, 0:1], 1.0 / V_SCALE, ALU.mult, ALU.mult)\
                  .then_inc(s_wout, 1)
                ve.wait_ge(s_pe0, 1)
                ve.tensor_copy(gain[:], score[0][:].rearrange("p a b -> p (a b)")).then_inc(s_setup, 1)
                ve.tensor_copy(clamp[:], bank[0][:, 0:KH]).then_inc(s_setup, 1)
                ve.wait_ge(s_pe0, 2)
                ve.tensor_copy(a_t[:, 0, :], bank[1][:, 0:P]).then_inc(s_setup, 1)
                ve.tensor_copy(a_t[:, 1, :], bank[1][:, P:2 * P]).then_inc(s_setup, 1)
                ve.wait_ge(s_pe0, 3)
                ve.tensor_copy(bias_all[:], bank[0][:, 0:P]).then_inc(s_setup, 1)
                ve.wait_ge(s_pe0, 4)
                ve.tensor_scalar(mix[:], bank[1][:, 0:P], 1.0 / D, None, ALU.mult).then_inc(s_setup, 1)

            def stats(k, batch, src, st, mv):
                for t in range(T):
                    ve.bn_stats(st[:, t, :], src[:, t, :]).then_inc(st_done[k], 1)
                for t in range(T):
                    wait_apart(ve, st_done[k], T * batch + t + 1, ve_steps)
                    ve.bn_aggr(mv[:, t, :], st[:, t, :]).then_inc(mv_done[k], 1)

            def apply(dst, src, mv, rs, done):
                for t in range(T):
                    ve.tensor_scalar(dst[:, t, :], src[:, t, :], mv[:, t, 0:1], rs[:, t:t + 1],
                                     ALU.subtract, ALU.mult).then_inc(done, 1)

            def stats_first(nb, npar):
                wait(ve, x_loaded[npar], 8 * nb + 16 - 8 * npar)
                wait(ve, xn_done, T * nb)
                stats(0, nb, xin[npar], st1, mv1)

            def norm_first(nb, npar):
                wait(ve, rs_done[0], nb + 1)
                wait(ve, xt_done, nb)
                apply(xn, xin[npar], mv1, rs1, xn_done)

            def sum_squares(nb, t):
                n = T * nb + t
                wait(ve, sqk_done, n + 1)
                ve.tensor_reduce(ssq[:, t % 2, QW // DH:], sqk[t % 2][:].rearrange("p (h d) -> p h d", d=DH),
                                 AX.X, ALU.add).then_inc(ssq_done, 1)
                wait(ve, sq_done, n + 1)
                ve.tensor_reduce(ssq[:, t % 2, 0:QW // DH], sq[:].rearrange("p (h d) -> p h d", d=DH),
                                 AX.X, ALU.add).then_inc(ssq_done, 1)

            def inverse_norms(nb, m):
                pair, step = 2 * nb + m, 0

                def then(ins):
                    nonlocal step
                    step += 1
                    ins.then_inc(rn_chain, 1)
                    wait(ve, rn_chain, RN_STEPS * pair + step)

                wait(ve, ssq_done, 4 * (pair + 1))
                then(ve.tensor_scalar(ssg[:], ssq[:].rearrange("p t h -> p (t h)"), norm_floor[:, 0:1],
                                      QK_SCALE ** -2, ALU.max, ALU.mult))
                ve.tensor_scalar(ssh[:], ssg[:], -0.5, None, ALU.mult)
                then(ve.tensor_scalar(bits[:], ssg[:].bitcast(INT32), 1, None, ALU.logical_shift_right))
                y = rn[:].rearrange("p t h -> p (t h)")
                then(ve.tensor_scalar(y.bitcast(INT32), bits[:], -1.0, float(0x5F3759DF), ALU.mult, ALU.add))
                for k in range(3):
                    then(ve.tensor_tensor(ysq[:], y, y, ALU.mult))
                    then(ve.tensor_tensor(yxx[:], ysq[:], ssh[:], ALU.mult))
                    then(ve.scalar_tensor_tensor(out=y, in0=yxx[:], scalar=1.5, in1=y, op0=ALU.add,
                                                 op1=ALU.mult))

            def norm_qk(nb, t):
                n = T * nb + t
                wait(ve, lo_done, 2 * n)
                nq = QW // DH
                r = rn[:, t % 2].rearrange("p (h o) -> p h o", o=1)
                ve.tensor_tensor(qn[:].rearrange("p (h d) -> p h d", d=DH),
                                 raw[t % 2][:, 0:QW].rearrange("p (h d) -> p h d", d=DH),
                                 r[:, 0:nq].broadcast_to([P, nq, DH]), ALU.mult).then_inc(qn_done, 1)
                ve.tensor_tensor(kn[:].rearrange("p (h d) -> p h d", d=DH),
                                 raw[t % 2][:, QW:].rearrange("p (h d) -> p h d", d=DH),
                                 r[:, nq:].broadcast_to([P, KH, DH]), ALU.mult).then_inc(qn_done, 1)

            def x_low(nb):
                wait(ve, xt_copied, nb + 1)
                wait(ve, pj_done, 16 * nb)
                ve.scalar_tensor_tensor(out=xT_lo[:], in0=bank[0][:], scalar=X_SCALE, in1=xT_hi[:],
                                        op0=ALU.mult, op1=ALU.subtract).then_inc(xlo_copied, 1)

            def split_p(b, h):
                q = KH * b + h
                wait(ve, mask_done, 3 * (q + 1))
                wait(ve, av_done, q)
                ve.tensor_copy(p_hi[:], prob[h % 2][:]).then_inc(phi_done, 1)
                wait(ve, phi_done, q + 1)
                ve.tensor_tensor(p_lo[:, 0:P_DVE], prob[h % 2][:, 0:P_DVE], p_hi[:, 0:P_DVE], ALU.subtract)\
                  .then_inc(plo_done, 1)

            def split_k(nb, t):
                n = T * nb + t
                k = kn[:].rearrange("p (h d) -> p h d", d=DH)
                wait(ve, qn_done, 2 * n + 2)
                wait(ve, tr_done, TR * (n - 1))
                ve.tensor_copy(ks[t % 2][:, :, 0], k).then_inc(hi_done, 1)
                ve.tensor_copy(ks[t % 2][:, :, 2], k).then_inc(hi_done, 1)
                wait(ve, hi_done, 3 * n + 1)
                ve.tensor_tensor(ks[t % 2][:, :, 1], k, ks[t % 2][:, :, 0], ALU.subtract)\
                  .then_inc(lo_done, 1)

            def split_q(nb, t):
                n = T * nb + t
                q = qn[:].rearrange("p (h d) -> p h d", d=DH)
                wait(ve, qg_done, n + 1)
                ve.tensor_copy(qs[t % 2][:, :, 0], q).then_inc(hi_done, 1)
                wait(ve, hi_done, 3 * n + 3)
                ve.tensor_tensor(qs[t % 2][:, :, 1], q, qs[t % 2][:, :, 0], ALU.subtract)\
                  .then_inc(lo_done, 1)

            def weigh(b, par, h):
                q = KH * b + h
                wait(ve, av_done, q + 1)
                wait(ve, og_done, q)
                ve.reciprocal(rden[:], acc_o[:, :, :, DH]).then_inc(rden_done, 1)
                wait(ve, rden_done, q + 1)
                wait(ve, o_done, q)
                ve.tensor_tensor(og[:], acc_o[:, :, :, 0:DH],
                                 rden[:].rearrange("p g (t o) -> p g t o", o=1).broadcast_to([P, G, T, DH]),
                                 ALU.mult).then_inc(og_done, 1)
                wait(ve, og_done, q + 1)
                if h == 0:
                    wait(ve, ot_done, T * b)
                ve.tensor_tensor(otok[:, :, h * DH:(h + 1) * DH], og[:, 0], og[:, 1], ALU.add)\
                  .then_inc(o_done, 1)

            def attn_stats(p):
                wait(ve, op_copied, p + 1)
                stats(1, p, attn, ln[0][0], ln[0][1])

            def x1_stats(p):
                wait(ve, x1_done, p + 1)
                stats(2, p, x1, ln[1][0], ln[1][1])

            def mix_out(p):
                wait(ve, ff_done, p + 1)
                ve.tensor_tensor(y[:], bank[1][:].rearrange("p (t d) -> p t d", d=D),
                                 bias_all[:].rearrange("p (o d) -> p o d", o=1).broadcast_to([P, T, D]),
                                 ALU.add).then_inc(y_done, 1)
                wait(ve, y_done, p + 1)
                stats(3, p, y, ln[2][0], ln[2][1])

            def iteration(b, par, prep, post, ahead):
                nb = b + 1
                for h in range(KH):
                    if prep and h == 0:
                        x_low(nb)
                    if post and h == 6:
                        mix_out(b - 1)
                    if h >= 2:
                        weigh(b, par, h - 2)
                    elif post:
                        weigh(b - 1, 1 - par, KH - 2 + h)
                    if h >= 1:
                        split_p(b, h - 1)
                    elif post:
                        split_p(b - 1, KH - 1)
                    if ahead and h == 7:
                        norm_first(b + 2, par)
                    if prep and h in (2, 3, 5, 6):
                        t = {2: 0, 3: 1, 5: 2, 6: 3}[h]
                        split_k(nb, t)
                        split_q(nb, t)
                    if post and h == 3:
                        attn_stats(b - 1)
                    if prep and h in (2, 5):
                        norm_qk(nb, {2: 1, 5: 3}[h])
                    if prep and h < T:
                        sum_squares(nb, h)
                    if prep and h in (1, 4):
                        inverse_norms(nb, h // 4)
                        norm_qk(nb, 2 * (h // 4))
                    if post and h == 4:
                        x1_stats(b - 1)
                    if ahead and h == 6:
                        stats_first(b + 2, par)

            ve.wait_ge(s_const, 8)
            stats_first(0, 0)
            setup()
            norm_first(0, 0)
            x_low(0)
            for m in range(2):
                sum_squares(0, 2 * m)
                sum_squares(0, 2 * m + 1)
                inverse_norms(0, m)
                for t in (2 * m, 2 * m + 1):
                    norm_qk(0, t)
                    split_k(0, t)
                    split_q(0, t)
            stats_first(1, 1)
            norm_first(1, 1)
            batches(ve, iteration)
            weigh(B - 1, (B - 1) % 2, KH - 2)
            split_p(B - 1, KH - 1)
            weigh(B - 1, (B - 1) % 2, KH - 1)
            attn_stats(B - 1)
            x1_stats(B - 1)
            mix_out(B - 1)


_INS = ["L0_attn_tokens", "L0_attn_norm_w", "L0_attn_Wq", "L0_attn_Wkv", "L0_attn_Wout",
        "L0_attn_q_gamma", "L0_attn_k_gamma", "L0_ffn_w_freq_real", "L0_ffn_w_freq_imag", "L0_ffn_bias"]


def kernel(**inputs):
    import numpy as _np
    import concourse.bacc as _bacc
    from concourse import mybir as _mybir
    from concourse.bass_utils import run_bass_kernel_spmd as _run

    nc = _bacc.Bacc("TRN2", target_bir_lowering=False, num_devices=1)
    arrays, args = {}, []
    for name in _INS:
        a = _np.ascontiguousarray(inputs[name])
        arrays[f"in_{name}_dram"] = a
        args.append(nc.dram_tensor(f"in_{name}_dram", a.shape, _mybir.dt.from_np(a.dtype), kind="ExternalInput").ap())
    angle = 2 * _np.pi / 128 * (_np.outer(_np.arange(128), _np.arange(128)) % 128)
    table = _np.stack([_np.cos(angle), _np.sin(angle), -_np.sin(angle)]).astype(_np.float32)
    arrays["dft_dram"] = table
    args.append(nc.dram_tensor("dft_dram", table.shape, _mybir.dt.float32, kind="ExternalInput").ap())
    o = nc.dram_tensor("out_0_dram", (8, 512, 128), _mybir.dt.float32, kind="ExternalOutput").ap()
    build(nc, *args, o)
    r = _run(nc, [arrays], core_ids=[0])
    return r.results[0]["out_0_dram"]
```

```python
import concourse.bass as bass
from concourse import mybir
from contextlib import ExitStack

FP32 = mybir.dt.float32
FP16 = mybir.dt.float16
INT32 = mybir.dt.int32
ALU = mybir.AluOpType
ACT = mybir.ActivationFunctionType
AX = mybir.AxisListType

P = 128
B, N, D = 8, 512, 128
KH, G, DH = 8, 2, 64
T = N // P
QW, KW = KH * G * DH, KH * DH
X_SCALE, W_SCALE = 64.0, 1024.0
V_SCALE = X_SCALE
EXP_BIAS = 4.5
QK_SCALE = 256.0
EPS_LN, EPS_RMS = 1e-5, 1.1920928955078125e-07
SOFTCLAMP = 50.0
UNITS = 3
P_AT = [[0, 512], [1024, 1408], [1792, 2176], [2048, 2432]]
P_LEN = 2560
P_DVE = 1792
RN_STEPS = 3 + 3 * 3
SQUARES_AT = {0: 0, 1: 1, 3: 2, 4: 3}
SPLIT_AT = {2: 0, 3: 1, 5: 2, 6: 3}
PJ, TR = 4, 4


def wait(eng, sem, value):
    if isinstance(value, int) and value <= 0:
        return
    eng.wait_ge(sem, value)


def wait_apart(eng, sem, value, steps):
    wait(eng, sem, value)
    if not isinstance(value, int):
        eng.sem_inc(steps, 1)


def build(nc, x, norm_w, wq, wkv, wout, q_gamma, k_gamma, w_real, w_imag, bias, dft, out):
    x_t = x.rearrange("b (t p) d -> b p t d", p=P)
    out_t = out.rearrange("b (t p) d -> b p t d", p=P)
    ctx = ExitStack()
    with ctx:
        def sb(name, shape, dtype=FP32):
            return ctx.enter_context(nc.sbuf_tensor(name, shape, dtype))

        def sem(name):
            return ctx.enter_context(nc.semaphore(name))

        w_hi = sb("w_hi", [P, QW + 2 * KW], FP16)
        w_lo = sb("w_lo", [P, QW + 2 * KW], FP16)
        w_top = sb("w_top", [P, 1]); w_max = sb("w_max", [1, 1]); w_guard = sb("w_guard", [1, 1])
        w_big = sb("w_big", [P, 1])
        w_unit = sb("w_unit", [P, 1]); w_unit2 = sb("w_unit2", [P, 1])
        norm_floor = sb("norm_floor", [P, 1])
        exp_bias = sb("exp_bias", [P, 1])
        w_out = sb("w_out", [P, 4, D])
        nw_col = sb("nw_col", [P, 1])
        mix = sb("mix", [P, P])
        bias_row = sb("bias_row", [1, P])[:]
        ones_row = sb("ones_row", [1, P])
        ident = sb("ident", [P, P])
        ident16 = sb("ident16", [P, P], FP16)
        ones8 = sb("ones8", [KH, P])
        g8m = sb("g8m", [KH, 1]); g8g = sb("g8g", [KH, 1]); g8r = sb("g8r", [KH, 1])
        m8b = sb("m8b", [KH, KH])
        gain = sb("gain", [P, QW])
        clamp = sb("clamp", [P, KH])
        minus_half = sb("minus_half", [P, T])
        xin = [sb(f"xin{i}", [P, T, D]) for i in range(2)]
        xn = sb("xn", [P, T, D])
        xT_hi = sb("xT_hi", [P, T * P], FP16)
        xT_lo = sb("xT_lo", [P, T * P], FP16)
        st1 = sb("st1", [P, T, 6]); mv1 = sb("mv1", [P, T, 2]); ve1 = sb("ve1", [P, T]); rs1 = sb("rs1", [P, T])
        raw = [sb(f"raw{i}", [P, QW + KW]) for i in range(2)]
        sq = sb("sq", [P, QW])
        sqk = [sb(f"sqk{i}", [P, KW]) for i in range(2)]
        ssq = sb("ssq", [P, 2, 24])
        ssg = sb("ssg", [P, 48]); ssh = sb("ssh", [P, 48]); ysq = sb("ysq", [P, 48]); yxx = sb("yxx", [P, 48])
        bits = sb("bits", [P, 48], INT32)
        rn = sb("rn", [P, 2, 24])
        qn = sb("qn", [P, QW])
        kn = sb("kn", [P, KW])
        qs = [sb(f"qs{i}", [P, KH * G, 2, DH], FP16) for i in range(2)]
        ks = [sb(f"ks{i}", [P, KH, 3, DH], FP16) for i in range(2)]
        qT = [sb(f"qT{i}", [P, KH * G, N], FP16) for i in range(2)]
        kT = [sb(f"kT{i}", [P, KH * 2, N], FP16) for i in range(2)]
        vf = [sb(f"vf{i}", [P, KH, DH]) for i in range(2)]
        vs = [sb(f"vs{i}", [P, T, KH, 2 * DH + 2], FP16) for i in range(2)]
        prob = [sb(f"prob{i}", [P, P_LEN]) for i in range(2)]
        p_hi = sb("p_hi", [P, P_LEN], FP16)
        p_lo = sb("p_lo", [P, P_LEN], FP16)
        small = [sq[0:KH, k * P:(k + 1) * P] for k in range(6)]
        gq8, gk8, gk8p = (a.rearrange("p (g d) -> p g d", g=G) for a in small[:3])
        g8, g8a, g8n = small[3:]
        g8b = qn[0:KH, :].rearrange("p (h d) -> p h d", h=KH)
        tables = raw[1][:, 0:3 * P].rearrange("p (k n) -> p k n", k=3)
        wf = raw[1][:, 3 * P:5 * P].rearrange("p (k n) -> p k n", k=2)
        a_t = raw[1][:, 5 * P:7 * P].rearrange("p (k n) -> p k n", k=2)
        w_all = prob[0][:, 0:QW + 2 * KW]
        w_abs = prob[1][:, 0:QW + 2 * KW]
        rden = sb("rden", [P, G, T])
        og = sb("og", [P, G, T, DH])
        otok = sb("otok", [P, T, KW])
        oT = sb("oT", [P, T, 4, P])
        attn = sb("attn", [P, T, D])
        xres = sb("xres", [P, T, D])
        z2 = sb("z2", [P, T, D])
        x1 = xres
        xn3 = z2
        x3T = sb("x3T", [P, T * P])
        y = attn
        z4 = z2
        res = z2
        ln = [[sb(f"ln{k}_{i}", [P, T, w] if w > 1 else [P, T]) for i, w in enumerate((6, 2, 1, 1))]
              for k in range(3)]

        score = [ctx.enter_context(nc.psum_tensor(f"score{i}", [P, 2, 512], FP32)) for i in range(2)]
        acc = ctx.enter_context(nc.psum_tensor("acc", [P, G, 512], FP32))
        bank = [ctx.enter_context(nc.psum_tensor(f"bank{i}", [P, 512], FP32)) for i in range(2)]
        bank16 = [bk[:].bitcast(FP16) for bk in bank]
        acc_o = acc[:, :, 0:T * (DH + 1)].rearrange("p g (t c) -> p g t c", c=DH + 1)

        s_const = sem("s_const"); s_setup = sem("s_setup"); s_gp = sem("s_gp"); s_pe0 = sem("s_pe0")
        s_w = sem("s_w"); s_tab = sem("s_tab"); s_g = sem("s_g"); s_g8 = sem("s_g8"); s_wabs = sem("s_wabs"); s_wout = sem("s_wout")
        ve_steps = sem("ve_steps"); gp_steps = sem("gp_steps")
        x_loaded = [sem("x_even_loaded"), sem("x_odd_loaded")]; r_loaded = sem("r_loaded"); res_free = sem("res_free")
        st_done = [sem(f"st{k}_done") for k in range(4)]
        mv_done = [sem(f"mv{k}_done") for k in range(4)]
        ve_done = [sem(f"ve{k}_done") for k in range(4)]
        rs_done = [sem(f"rs{k}_done") for k in range(4)]
        xn_done = sem("xn_done"); xt_done = sem("xt_done"); xt_copied = sem("xt_copied")
        pj_done = sem("pj_done"); pj_copied = sem("pj_copied")
        vhi_done = sem("vhi_done"); sq_done = sem("sq_done"); sqk_done = sem("sqk_done"); ssq_done = sem("ssq_done"); rn_chain = sem("rn_chain")
        qn_done = sem("qn_done"); qg_done = sem("qg_done")
        xlo_copied = sem("xlo_copied"); vlo_done = sem("vlo_done")
        phi_done = sem("phi_done"); plo_done = sem("plo_done"); s_wn = sem("s_wn"); s_wp = sem("s_wp")
        hi_done = sem("hi_done"); lo_done = sem("lo_done")
        tr_done = sem("tr_done"); tr_copied = sem("tr_copied")
        s_done = sem("s_done"); tanh_done = sem("tanh_done"); exp_done = sem("exp_done")
        mask_done = sem("mask_done"); av_done = sem("av_done")
        rden_done = sem("rden_done"); og_done = sem("og_done"); o_done = sem("o_done")
        ot_done = sem("ot_done"); ot_copied = sem("ot_copied"); op_done = sem("op_done")
        op_copied = sem("op_copied"); z2_done = sem("z2_done"); x1_done = sem("x1_done")
        xn3_done = sem("xn3_done"); ft_done = sem("ft_done"); ft_copied = sem("ft_copied")
        ff_done = sem("ff_done"); y_done = sem("y_done"); z4_done = sem("z4_done")
        res_done = sem("res_done")

        block = ctx.enter_context(nc.Block())

        def batches(eng, iteration):
            iteration(0, 0, True, False, True)
            with eng.Fori(1, B - 3, 2) as b:
                iteration(b, 1, True, True, True)
                iteration(b + 1, 0, True, True, True)
            iteration(B - 3, 1, True, True, True)
            iteration(B - 2, 0, True, True, False)
            iteration(B - 1, 1, False, True, False)

        @block.sync
        def _(sp):
            sp.sem_inc(res_free, 16)
            sp.dma_start(xin[0][:], x_t[0]).then_inc(x_loaded[0], 16)
            sp.dma_start(prob[0][:, 0:QW], wq).then_inc(s_w, 16)
            sp.dma_start(prob[0][:, QW:QW + 2 * KW], wkv).then_inc(s_w, 16)
            sp.dma_start(nw_col[:], norm_w.rearrange("(d o) -> d o", o=1)).then_inc(s_w, 16)
            sp.dma_start(xin[1][:], x_t[1]).then_inc(x_loaded[1], 16)
            sp.dma_start(gq8, q_gamma.rearrange("(h g) d -> h g d", g=G)).then_inc(s_g, 16)
            for g in range(G):
                sp.dma_start(gk8[:, g, :], k_gamma).then_inc(s_g, 16)
            sp.dma_start(w_out[:], wout.rearrange("(c p) d -> p c d", p=P)).then_inc(s_tab, 16)
            sp.dma_start(tables, dft.rearrange("k p d -> p k d")).then_inc(s_tab, 16)
            sp.dma_start(wf[:, 0, :], w_real).then_inc(s_tab, 16)
            sp.dma_start(wf[:, 1, :], w_imag).then_inc(s_tab, 16)
            sp.dma_start(bias_row, bias.rearrange("(o d) -> o d", o=1)).then_inc(s_tab, 16)

            def load_next(b, par):
                wait(sp, xn_done, T * (b + 1))
                sp.dma_start(xin[par][:], x_t[b + 2]).then_inc(x_loaded[par], 16)

            def load_residual(b):
                wait(sp, res_done, b)
                sp.dma_start(xres[:], x_t[b]).then_inc(r_loaded, 16)

            def store(p):
                wait(sp, res_done, p + 1)
                sp.dma_start(out_t[p], res[:]).then_inc(res_free, 16)

            def iteration(b, par, prep):
                if prep:
                    load_next(b, par)
                load_residual(b)
                if not (isinstance(b, int) and b == 0):
                    store(b - 1)

            iteration(0, 0, True)
            with sp.Fori(1, B - 3, 2) as b:
                iteration(b, 1, True)
                iteration(b + 1, 0, True)
            iteration(B - 3, 1, True)
            iteration(B - 2, 0, False)
            iteration(B - 1, 1, False)
            store(B - 1)
            sp.wait_ge(res_free, 16 * (B + 1))

        @block.tensor
        def _(pe):
            cos, sin, msin = (tables[:, k, :] for k in range(3))
            wr, wi = wf[:, 0, :], wf[:, 1, :]

            def setup():
                pe.wait_ge(s_const, 8)
                pe.wait_ge(s_wn, 2)
                pe.transpose(score[1][0:1, 0, 0:P], w_top[:], ident[:]).then_inc(s_wp, 1)
                pe.wait_ge(s_wn, 4)
                pe.matmul(score[1][:, 1, 0:1], ones_row[:], w_guard[:], start=True, stop=True).then_inc(s_wp, 1)
                pe.wait_ge(s_g8, 8)
                for c in range(2):
                    pe.matmul(score[0][:, c, :], ones8[:], g8b[:, 4 * c:4 * c + 4, :].rearrange("p h d -> p (h d)"),
                              start=True, stop=True)
                pe.matmul(acc[:, 1, P:P + KH], ones8[:], m8b[:], start=True, stop=True).then_inc(s_pe0, 1)
                x_transpose(0)
                pe.wait_ge(s_tab, 80)
                pe.matmul(acc[:, 0, 0:P], wr, cos, start=True, stop=False)
                pe.matmul(acc[:, 0, 0:P], wi, sin, start=False, stop=True)
                pe.matmul(acc[:, 0, P:2 * P], wi, cos, start=True, stop=False)
                pe.matmul(acc[:, 0, P:2 * P], wr, msin, start=False, stop=True).then_inc(s_pe0, 1)

            def setup_mix():
                pe.wait_ge(s_setup, 5)
                pe.matmul(acc[:, 1, 0:P], a_t[:, 0, :], cos, start=True, stop=False)
                pe.matmul(acc[:, 1, 0:P], a_t[:, 1, :], msin, start=False, stop=True).then_inc(s_pe0, 1)

            def x_transpose(nb):
                wait(pe, tr_copied, TR * T * nb - 1)
                wait(pe, xn_done, T * (nb + 1))
                for t in range(T):
                    mm = pe.transpose(bank[0][:, t * P:(t + 1) * P], xn[:, t, :], ident[:])
                mm.then_inc(xt_done, 1)

            def project(nb, t, looped, post, half):
                n, p = T * nb + t, nb - 2
                if t == 0:
                    wait(pe, xt_copied, nb + 1)
                    wait(pe, xlo_copied, nb + 1)
                for c in (2 * half, 2 * half + 1):
                    if c >= 2:
                        wait(pe, pj_copied, PJ * n + c - 1)
                    elif t == 0:
                        wait(pe, tr_copied, 16 * nb)
                    elif post and t == 2:
                        wait(pe, *((op_copied, p + 1), (ot_copied, T * (p + 1)))[c])
                    elif looped and t == 3:
                        wait(pe, tr_copied, TR * T * nb + 3 + c)
                    else:
                        wait(pe, pj_copied, PJ * n - 1 + c)
                    tile, cols = slice(t * P, (t + 1) * P), slice(c * 512, (c + 1) * 512)
                    pe.matmul(bank[c % 2][:], xT_hi[:, tile], w_hi[:, cols], start=True, stop=False)
                    pe.matmul(bank[c % 2][:], xT_hi[:, tile], w_lo[:, cols], start=False, stop=False)
                    pe.matmul(bank[c % 2][:], xT_lo[:, tile], w_hi[:, cols], start=False, stop=False)
                    pe.matmul(bank[c % 2][:], xT_lo[:, tile], w_lo[:, cols], start=False, stop=True)\
                      .then_inc(pj_done, 1)

            def transposes(nb, t, looped, post, half):
                n, p = T * nb + t, nb - 2
                wait(pe, lo_done, 2 * (n + 1))
                for c in (2 * half, 2 * half + 1):
                    if c >= 2:
                        wait(pe, tr_copied, TR * n + c - 1)
                    elif t == 0:
                        wait(pe, pj_copied, PJ * (n + (2 if looped else 3)) + 3 + c)
                    elif looped and t == 1:
                        wait(pe, pj_copied, PJ * (n + 2) + 3 + c)
                    elif post and t == 2:
                        wait(pe, *((ft_copied, p + 1), (y_done, p + 1))[c])
                    else:
                        wait(pe, tr_copied, TR * n - 1 + c)
                    for k in range(8):
                        h, half = 4 * (c - 2) + k // 2, k % 2
                        src = qs[t % 2][:, 8 * c + k] if c < 2 else ks[t % 2][:, h, half:half + 2]
                        mm = pe.transpose(bank16[c % 2][:, k * P:(k + 1) * P],
                                          src.rearrange("p s d -> p (s d)"), ident16[:])
                    mm.then_inc(tr_done, 1)

            def scores(b, par, h, u):
                q = KH * b + h
                if h == 0 and u == 0:
                    wait(pe, tr_copied, 16 * (b + 1))
                wait(pe, tanh_done, UNITS * q + u - 1)
                s = score[(UNITS * h + u) % 2]
                for j, at in (((0, 0),), ((1, 0),), ((2, 0), (3, 256)))[u]:
                    for half in range(2):
                        for g in range(G):
                            mm = pe.matmul(s[:, g, at:at + N - j * P], kT[par][:, 2 * h + half, j * P:(j + 1) * P],
                                           qT[par][:, G * h + g, j * P:N], start=(half == 0), stop=(half == 1))
                mm.then_inc(s_done, 1)

            def values(b, par, h, g):
                q = KH * b + h
                if g == 0:
                    if h == 0:
                        wait(pe, vhi_done, T * (b + 1))
                        wait(pe, vlo_done, T * (b + 1))
                    wait(pe, og_done, q)
                    wait(pe, plo_done, 2 * (q + 1))
                for t in range(T):
                    o = acc[:, g, t * (DH + 1):(t + 1) * (DH + 1)]
                    for j in range(t + 1):
                        at = P_AT[j][g] + (t - j) * P
                        for k, pr in enumerate((p_hi, p_lo)):
                            pe.matmul(o, pr[:, at:at + P], vs[par][:, j, h, 0:DH + 1],
                                      start=(j == 0 and k == 0), stop=False)
                            mm = pe.matmul(o[:, 0:DH], pr[:, at:at + P], vs[par][:, j, h, DH + 2:],
                                           start=False, stop=(j == t and k == 1))
                if g == G - 1:
                    mm.then_inc(av_done, 1)

            def o_transposes(p, prep, half):
                if half == 0:
                    wait(pe, o_done, KH * (p + 1))
                for t in (2 * half, 2 * half + 1):
                    if half == 1:
                        wait(pe, ot_copied, T * p + t - 1)
                    elif prep:
                        wait(pe, pj_copied, PJ * (T * (p + 2) + 1) + 3 + t)
                    for c in range(4):
                        mm = pe.transpose(bank[t % 2][:, c * P:(c + 1) * P],
                                          otok[:, t, c * P:(c + 1) * P], ident[:])
                    mm.then_inc(ot_done, 1)

            def out_project(p):
                if isinstance(p, int) and p == 0:
                    pe.wait_ge(s_wout, 1)
                wait(pe, ot_copied, T * (p + 1))
                for t in range(T):
                    for c in range(4):
                        mm = pe.matmul(bank[0][:, t * P:(t + 1) * P], oT[:, t, c, :], w_out[:, c, :],
                                       start=(c == 0), stop=(c == 3))
                mm.then_inc(op_done, 1)

            def f_transpose(p, prep):
                wait(pe, xn3_done, T * (p + 1))
                if prep:
                    wait(pe, tr_copied, TR * (T * (p + 2) + 1) + 3)
                for t in range(T):
                    mm = pe.transpose(bank[0][:, t * P:(t + 1) * P], xn3[:, t, :], ident[:])
                mm.then_inc(ft_done, 1)

            def f_mix(p, prep):
                wait(pe, ft_copied, p + 1)
                if prep:
                    wait(pe, tr_copied, TR * (T * (p + 2) + 1) + 4)
                for t in range(T):
                    o = bank[1][:, t * P:(t + 1) * P]
                    pe.matmul(o, x3T[:, t * P:(t + 1) * P], mix[:], start=True, stop=False)
                    mm = pe.matmul(o, ones_row[:], bias_row, start=False, stop=True)
                mm.then_inc(ff_done, 1)

            def extra(b, h, place, prep, post, ahead):
                nb, p = b + 1, b - 1
                if ahead and (h, place) == (7, 3):
                    x_transpose(b + 2)
                if prep and h == 0 and place in (1, 2):
                    project(nb, 0, True, post, place - 1)
                if prep and h == 1 and place < 2:
                    project(nb, 1, True, post, place)
                if prep and h in (2, 3) and place >= 2:
                    project(nb, h, True, post, place - 2)
                if post and h == 1 and place >= 2:
                    o_transposes(p, prep, place - 2)
                if post and (h, place) == (2, 0):
                    out_project(p)
                if prep and h in (3, 4) and place < 2:
                    transposes(nb, h - 3, True, post, place)
                if post and (h, place) == (5, 3):
                    f_transpose(p, prep)
                if post and (h, place) == (6, 0):
                    f_mix(p, prep)
                if prep and h == 6 and place >= 2:
                    transposes(nb, 2, True, post, place - 2)
                if prep and h == 7 and place < 2:
                    transposes(nb, 3, True, post, place)

            def iteration(b, par, prep, post, ahead):
                for h in range(KH):
                    for u in range(UNITS):
                        scores(b, par, h, u)
                        extra(b, h, u, prep, post, ahead)
                    for g in range(G):
                        if h >= 1:
                            values(b, par, h - 1, g)
                        elif post:
                            values(b - 1, 1 - par, KH - 1, g)
                        if g == 0:
                            extra(b, h, 3, prep, post, ahead)

            setup()
            pe.wait_ge(s_setup, 2)
            for t in range(T):
                for half in range(2):
                    project(0, t, False, False, half)
                if t == 0:
                    setup_mix()
            pe.wait_ge(s_setup, 7)
            for t in range(T):
                for half in range(2):
                    transposes(0, t, False, False, half)
            x_transpose(1)
            batches(pe, iteration)
            for g in range(G):
                values(B - 1, (B - 1) % 2, KH - 1, g)
            for half in range(2):
                o_transposes(B - 1, False, half)
            out_project(B - 1)
            f_transpose(B - 1, False)
            f_mix(B - 1, False)

        @block.scalar
        def _(act):
            def x_copy(nb):
                wait(act, xt_done, nb + 1)
                wait(act, pj_done, 16 * nb)
                act.activation(xT_hi[:], bank[0][:], ACT.Copy, scale=X_SCALE).then_inc(xt_copied, 1)

            def p_copy(nb, npar, t, half):
                n = T * nb + t
                for c in (2 * half, 2 * half + 1):
                    wait(act, pj_done, PJ * n + c + 1)
                    if c == 0:
                        wait(act, qn_done, 2 * (n - 1))
                    if c == 2:
                        wait(act, ssq_done, 2 * (n - 1))
                        act.activation(sqk[t % 2][:], bank[0][:], ACT.Square).then_inc(sqk_done, 1)
                    if c < 3:
                        act.copy(raw[t % 2][:, c * 512:(c + 1) * 512], bank[c % 2][:]).then_inc(pj_copied, 1)
                    else:
                        wait(act, vlo_done, n - 1)
                        act.activation(vf[t % 2][:].rearrange("p h d -> p (h d)"), bank[1][:],
                                       ACT.Copy, scale=1.0 / W_SCALE).then_inc(pj_copied, 1)

            def v_high(nb, npar, t):
                n = T * nb + t
                wait(act, pj_copied, PJ * n + 4)
                if t == 0:
                    wait(act, av_done, KH * (nb - 1))
                act.copy(vs[npar][:, t, :, 0:DH], vf[t % 2][:]).then_inc(vhi_done, 1)

            def t_copy(nb, npar, t, half):
                n = T * nb + t
                for c in (2 * half, 2 * half + 1):
                    wait(act, tr_done, TR * n + c + 1)
                    if c in (0, 2):
                        wait(act, s_done, 24 * (nb - 1))
                    dst = (qT if c < 2 else kT)[npar]
                    h = 8 * (c % 2)
                    act.copy(dst[:, h:h + 8, t * P:(t + 1) * P],
                             bank16[c % 2].rearrange("p (h n) -> p h n", n=P)).then_inc(tr_copied, 1)

            def o_copy(p, half):
                for t in (2 * half, 2 * half + 1):
                    wait(act, ot_done, T * p + t + 1)
                    act.copy(oT[:, t].rearrange("p c n -> p (c n)"), bank[t % 2][:]).then_inc(ot_copied, 1)

            def tanh(b, h, u):
                q = KH * b + h
                if u == 0:
                    wait(act, plo_done, 2 * (q - 1))
                wait(act, s_done, UNITS * q + u + 1)
                w = 512 if u == 0 else 384
                at = P_AT[u][0]
                act.activation(prob[h % 2][:, at:at + 2 * w].rearrange("p (g n) -> p g n", g=G),
                               score[(UNITS * h + u) % 2][:, :, 0:w], ACT.Tanh,
                               scale=clamp[:, h:h + 1]).then_inc(tanh_done, 1)

            def exp(b, h):
                q = KH * b + h
                wait(act, tanh_done, UNITS * (q + 1))
                act.activation(prob[h % 2][:], prob[h % 2][:], ACT.Exp, bias=exp_bias[:, 0:1],
                               scale=SOFTCLAMP * DH ** -0.5).then_inc(exp_done, 1)

            def attn_copy(p):
                wait(act, op_done, p + 1)
                act.copy(attn[:].rearrange("p t d -> p (t d)"), bank[0][:]).then_inc(op_copied, 1)

            def f_copy(p):
                wait(act, ft_done, p + 1)
                act.copy(x3T[:], bank[0][:]).then_inc(ft_copied, 1)

            def y_copy(p):
                wait(act, ff_done, p + 1)
                act.copy(y[:].rearrange("p t d -> p (t d)"), bank[1][:]).then_inc(y_done, 1)

            def extra(b, par, h, place, prep, post, ahead):
                nb, npar, p = b + 1, 1 - par, b - 1
                if ahead and (h, place) == (7, 3):
                    x_copy(b + 2)
                if prep and h == 0 and place in (1, 2):
                    p_copy(nb, npar, 0, place - 1)
                if prep and h == 1 and place < 2:
                    p_copy(nb, npar, 1, place)
                if prep and h in (2, 3) and place >= 2:
                    p_copy(nb, npar, h, place - 2)
                if prep and (h, place) in ((1, 3), (2, 1), (3, 3), (4, 2)):
                    v_high(nb, npar, h - 1)
                if post and h == 1 and place >= 2:
                    o_copy(p, place - 2)
                if post and (h, place) == (2, 0):
                    attn_copy(p)
                if prep and h in (3, 4) and place < 2:
                    t_copy(nb, npar, h - 3, place)
                if post and (h, place) == (5, 3):
                    f_copy(p)
                if post and (h, place) == (6, 0):
                    y_copy(p)
                if prep and h == 6 and place >= 2:
                    t_copy(nb, npar, 2, place - 2)
                if prep and h == 7 and place < 2:
                    t_copy(nb, npar, 3, place)

            def iteration(b, par, prep, post, ahead):
                for h in range(KH):
                    for u in range(UNITS):
                        tanh(b, h, u)
                        extra(b, par, h, u, prep, post, ahead)
                    exp(b, h)
                    extra(b, par, h, 3, prep, post, ahead)

            x_copy(0)
            for t in range(T):
                for half in range(2):
                    p_copy(0, 0, t, half)
                v_high(0, 0, t)
            for t in range(T):
                for half in range(2):
                    t_copy(0, 0, t, half)
            x_copy(1)
            batches(act, iteration)
            for half in range(2):
                o_copy(B - 1, half)
            attn_copy(B - 1)
            f_copy(B - 1)
            y_copy(B - 1)

        @block.gpsimd
        def _(gp):
            gp.memset(ident[:], 0.0).then_inc(s_gp, 1)
            gp.wait_ge(s_gp, 1)
            gp.affine_select(out=ident[:], in_=ident[:], compare_op=ALU.not_equal, fill=1.0, base=0,
                             pattern=[[-1, P]], channel_multiplier=1).then_inc(s_const, 1)
            gp.memset(minus_half[:], -0.5).then_inc(s_const, 1)
            gp.memset(ones_row[:], 1.0).then_inc(s_const, 1)
            gp.memset(ones8[:], 1.0).then_inc(s_const, 1)
            gp.memset(exp_bias[:], EXP_BIAS).then_inc(s_const, 1)
            gp.memset(ident16[:], 0.0).then_inc(s_gp, 1)
            gp.wait_ge(s_gp, 2)
            gp.affine_select(out=ident16[:], in_=ident16[:], compare_op=ALU.not_equal, fill=1.0, base=0,
                             pattern=[[-1, P]], channel_multiplier=1).then_inc(s_const, 1)
            for i in range(2):
                gp.memset(vs[i][:, :, :, DH:DH + 2], 1.0).then_inc(s_const, 1)

            def rstd(k, batch, ve, rs, mv, scale, eps):
                wait_apart(gp, mv_done[k], T * (batch + 1), gp_steps)
                gp.tensor_scalar(ve[:], mv[:, :, 1], scale, eps, ALU.mult, ALU.add).then_inc(ve_done[k], 1)
                wait(gp, ve_done[k], batch + 1)
                gp.tensor_tensor(rs[:], ve[:], minus_half[:, 0:T], ALU.pow).then_inc(rs_done[k], 1)

            def rstd_first(nb):
                rstd(0, nb, ve1, rs1, mv1, 1.0 + EPS_RMS, EPS_LN * EPS_RMS)

            def rstd_post(k, p):
                rstd(k, p, ln[k - 1][2], ln[k - 1][3], ln[k - 1][1], 1.0, EPS_LN)

            def squares(nb, t):
                n = T * nb + t
                wait(gp, pj_copied, PJ * n + 2)
                wait(gp, ssq_done, 2 * n)
                gp.tensor_tensor(sq[:], raw[t % 2][:, 0:QW], raw[t % 2][:, 0:QW], ALU.mult).then_inc(sq_done, 1)

            def gains(nb, t):
                n = T * nb + t
                wait(gp, qn_done, 2 * n + 1)
                gp.tensor_tensor(qn[:], qn[:], gain[:], ALU.mult).then_inc(qg_done, 1)

            def v_low(nb, npar, t):
                n = T * nb + t
                wait(gp, vhi_done, n + 1)
                gp.tensor_tensor(vs[npar][:, t, :, DH + 2:], vf[t % 2][:], vs[npar][:, t, :, 0:DH],
                                 ALU.subtract).then_inc(vlo_done, 1)

            def mask(b, h):
                q = KH * b + h
                wait_apart(gp, exp_done, q + 1, gp_steps)
                pr = prob[h % 2]
                blocks = (pr[:, 0:1024].rearrange("p (g n) -> p g n", g=G)[:, :, 0:P],
                          pr[:, 1024:2560].rearrange("p (j g n) -> p j g n", j=2, g=G)[:, :, :, 0:P],
                          pr[:, 1792:2560].rearrange("p (g n) -> p g n", g=G)[:, :, 256:256 + P])
                for k, blk in enumerate(blocks):
                    gp.affine_select(out=blk, in_=blk, compare_op=ALU.is_ge, fill=0.0, base=0,
                                     pattern=[[0, 2], [0, 2], [1, P]] if k == 1 else [[0, 2], [1, P]],
                                     channel_multiplier=-1).then_inc(mask_done, 1)

            def p_low(b, h):
                q = KH * b + h
                wait(gp, phi_done, q + 1)
                gp.tensor_tensor(p_lo[:, P_DVE:], prob[h % 2][:, P_DVE:], p_hi[:, P_DVE:], ALU.subtract)\
                  .then_inc(plo_done, 1)

            def first_residual(p):
                wait(gp, z2_done, T * (p + 1))
                wait(gp, r_loaded, 16 * (p + 1))
                gp.tensor_tensor(x1[:], z2[:], xres[:], ALU.add).then_inc(x1_done, 1)

            def second_residual(p):
                wait(gp, z4_done, T * (p + 1))
                gp.tensor_tensor(res[:], res[:], x1[:], ALU.add).then_inc(res_done, 1)

            def iteration(b, par, prep, post, ahead):
                for h in range(KH):
                    if post and h == 5:
                        rstd_post(2, b - 1)
                    if ahead and h == 7:
                        rstd_first(b + 2)
                    if prep and h in SPLIT_AT:
                        gains(b + 1, SPLIT_AT[h])
                    if h >= 1:
                        p_low(b, h - 1)
                    elif post:
                        p_low(b - 1, KH - 1)
                    if h in (5, 6):
                        mask(b, h)
                    if prep and h in SQUARES_AT:
                        squares(b + 1, SQUARES_AT[h])
                    if prep and 2 <= h <= 5:
                        v_low(b + 1, 1 - par, h - 2)
                    if post and h == 3:
                        rstd_post(1, b - 1)
                    if post and h == 4:
                        first_residual(b - 1)
                    if post and h == 7:
                        rstd_post(3, b - 1)
                    if h not in (5, 6):
                        mask(b, h)
                    if post and h == 7:
                        second_residual(b - 1)

            rstd_first(0)
            for m in range(2):
                for t in (2 * m, 2 * m + 1):
                    squares(0, t)
                    v_low(0, 0, t)
                gp.wait_ge(s_setup, 6)
                for t in (2 * m, 2 * m + 1):
                    gains(0, t)
            rstd_first(1)
            batches(gp, iteration)
            p_low(B - 1, KH - 1)
            rstd_post(1, B - 1)
            first_residual(B - 1)
            rstd_post(2, B - 1)
            rstd_post(3, B - 1)
            second_residual(B - 1)

        @block.vector
        def _(ve):
            def setup():
                ve.wait_ge(s_w, 48)
                ve.tensor_scalar(w_all, w_all, nw_col[:, 0:1], None, ALU.mult).then_inc(s_wn, 1)
                ve.wait_ge(s_wn, 1)
                ve.scalar_tensor_tensor(out=w_abs, in0=w_all, scalar=-1.0, in1=w_all, op0=ALU.mult,
                                        op1=ALU.max).then_inc(s_wabs, 1)
                ve.wait_ge(s_wabs, 1)
                ve.tensor_reduce(w_top[:], w_abs, AX.X, ALU.max).then_inc(s_wn, 1)
                ve.wait_ge(s_g, 48)
                ve.tensor_scalar(gk8p, gk8, 1.0, None, ALU.add).then_inc(s_g8, 1)
                ve.wait_ge(s_g8, 1)
                ve.scalar_tensor_tensor(out=g8.rearrange("p (g d) -> p g d", g=G), in0=gq8, scalar=1.0,
                                        in1=gk8p, op0=ALU.add, op1=ALU.mult).then_inc(s_g8, 1)
                ve.wait_ge(s_g8, 2)
                ve.scalar_tensor_tensor(out=g8a, in0=g8, scalar=-1.0, in1=g8, op0=ALU.mult,
                                        op1=ALU.max).then_inc(s_g8, 1)
                ve.wait_ge(s_g8, 3)
                ve.tensor_reduce(g8m[:], g8a, AX.X, ALU.max).then_inc(s_g8, 1)
                ve.wait_ge(s_g8, 4)
                ve.tensor_scalar(g8g[:], g8m[:], 1e-30, None, ALU.max).then_inc(s_g8, 1)
                ve.wait_ge(s_g8, 5)
                ve.reciprocal(g8r[:], g8g[:]).then_inc(s_g8, 1)
                ve.wait_ge(s_g8, 6)
                ve.tensor_scalar(g8n, g8, g8r[:, 0:1], None, ALU.mult).then_inc(s_g8, 1)
                ve.tensor_scalar(m8b[:], ident[0:KH, 0:KH], g8g[:, 0:1], DH / SOFTCLAMP / QK_SCALE ** 2,
                                 ALU.mult, ALU.mult)
                ve.wait_ge(s_g8, 7)
                ve.tensor_tensor(g8b, g8n.rearrange("p (o d) -> p o d", o=1).broadcast_to([KH, KH, P]),
                                 ident[0:KH, 0:KH].rearrange("p (h o) -> p h o", o=1)
                                 .broadcast_to([KH, KH, P]), ALU.mult).then_inc(s_g8, 1)
                norm_first(0, 0)
                ve.wait_ge(s_wp, 1)
                ve.tensor_reduce(w_max[:], score[1][0:1, 0, 0:P], AX.X, ALU.max).then_inc(s_wn, 1)
                ve.wait_ge(s_wn, 3)
                ve.tensor_scalar(w_guard[:], w_max[:], 1e-20, None, ALU.max).then_inc(s_wn, 1)
                ve.wait_ge(s_wp, 2)
                ve.tensor_copy(w_big[:], score[1][:, 1, 0:1]).then_inc(s_wn, 1)
                ve.wait_ge(s_wn, 5)
                ve.reciprocal(w_unit[:], w_big[:]).then_inc(s_wn, 1)
                ve.wait_ge(s_wn, 6)
                ve.tensor_scalar(w_all, w_all, w_unit[:, 0:1], W_SCALE, ALU.mult, ALU.mult).then_inc(s_wn, 1)
                ve.tensor_scalar(w_unit2[:], w_unit[:], 1e-12 * X_SCALE * W_SCALE, None, ALU.mult)\
                  .then_inc(s_wn, 1)
                ve.wait_ge(s_wn, 8)
                ve.tensor_tensor(norm_floor[:], w_unit2[:], w_unit2[:], ALU.mult).then_inc(s_setup, 1)
                ve.tensor_copy(w_hi[:], w_all).then_inc(s_wn, 1)
                ve.wait_ge(s_wn, 9)
                ve.tensor_tensor(w_lo[:], w_all, w_hi[:], ALU.subtract).then_inc(s_setup, 1)

            def setup_rest():
                ve.wait_ge(s_pe0, 2)
                ve.tensor_copy(clamp[:], acc[:, 1, P:P + KH]).then_inc(s_setup, 1)
                ve.tensor_copy(a_t[:, 0, :], acc[:, 0, 0:P]).then_inc(s_setup, 1)
                ve.tensor_copy(a_t[:, 1, :], acc[:, 0, P:2 * P]).then_inc(s_setup, 1)
                ve.tensor_copy(gain[:], score[0][:].rearrange("p a b -> p (a b)")).then_inc(s_setup, 1)
                ve.wait_ge(s_tab, 80)
                ve.tensor_scalar(w_out[:], w_out[:], w_big[:, 0:1], 1.0 / V_SCALE, ALU.mult, ALU.mult)\
                  .then_inc(s_wout, 1)
                ve.wait_ge(s_pe0, 3)
                ve.tensor_scalar(mix[:], acc[:, 1, 0:P], 1.0 / D, None, ALU.mult).then_inc(s_setup, 1)

            def stats(k, batch, src, st, mv):
                for t in range(T):
                    ve.bn_stats(st[:, t, :], src[:, t, :]).then_inc(st_done[k], 1)
                for t in range(T):
                    wait_apart(ve, st_done[k], T * batch + t + 1, ve_steps)
                    ve.bn_aggr(mv[:, t, :], st[:, t, :]).then_inc(mv_done[k], 1)

            def apply(dst, src, mv, rs, done):
                for t in range(T):
                    ve.tensor_scalar(dst[:, t, :], src[:, t, :], mv[:, t, 0:1], rs[:, t:t + 1],
                                     ALU.subtract, ALU.mult).then_inc(done, 1)

            def stats_first(nb, npar):
                wait(ve, x_loaded[npar], 8 * nb + 16 - 8 * npar)
                wait(ve, xn_done, T * nb)
                stats(0, nb, xin[npar], st1, mv1)

            def norm_first(nb, npar):
                wait(ve, rs_done[0], nb + 1)
                wait(ve, xt_done, nb)
                apply(xn, xin[npar], mv1, rs1, xn_done)

            def sum_squares(nb, t):
                n = T * nb + t
                wait(ve, sqk_done, n + 1)
                ve.tensor_reduce(ssq[:, t % 2, QW // DH:], sqk[t % 2][:].rearrange("p (h d) -> p h d", d=DH),
                                 AX.X, ALU.add).then_inc(ssq_done, 1)
                wait(ve, sq_done, n + 1)
                ve.tensor_reduce(ssq[:, t % 2, 0:QW // DH], sq[:].rearrange("p (h d) -> p h d", d=DH),
                                 AX.X, ALU.add).then_inc(ssq_done, 1)

            def inverse_norms(nb, m):
                pair, step = 2 * nb + m, 0

                def then(ins):
                    nonlocal step
                    step += 1
                    ins.then_inc(rn_chain, 1)
                    wait(ve, rn_chain, RN_STEPS * pair + step)

                wait(ve, ssq_done, 4 * (pair + 1))
                then(ve.tensor_scalar(ssg[:], ssq[:].rearrange("p t h -> p (t h)"), norm_floor[:, 0:1],
                                      QK_SCALE ** -2, ALU.max, ALU.mult))
                ve.tensor_scalar(ssh[:], ssg[:], -0.5, None, ALU.mult)
                then(ve.tensor_scalar(bits[:], ssg[:].bitcast(INT32), 1, None, ALU.logical_shift_right))
                y = rn[:].rearrange("p t h -> p (t h)")
                then(ve.tensor_scalar(y.bitcast(INT32), bits[:], -1.0, float(0x5F3759DF), ALU.mult, ALU.add))
                for k in range(3):
                    then(ve.tensor_tensor(ysq[:], y, y, ALU.mult))
                    then(ve.tensor_tensor(yxx[:], ysq[:], ssh[:], ALU.mult))
                    then(ve.scalar_tensor_tensor(out=y, in0=yxx[:], scalar=1.5, in1=y, op0=ALU.add,
                                                 op1=ALU.mult))

            def norm_qk(nb, t):
                n = T * nb + t
                wait(ve, lo_done, 2 * n)
                nq = QW // DH
                r = rn[:, t % 2].rearrange("p (h o) -> p h o", o=1)
                ve.tensor_tensor(qn[:].rearrange("p (h d) -> p h d", d=DH),
                                 raw[t % 2][:, 0:QW].rearrange("p (h d) -> p h d", d=DH),
                                 r[:, 0:nq].broadcast_to([P, nq, DH]), ALU.mult).then_inc(qn_done, 1)
                wait(ve, pj_copied, PJ * n + 3)
                ve.tensor_tensor(kn[:].rearrange("p (h d) -> p h d", d=DH),
                                 raw[t % 2][:, QW:].rearrange("p (h d) -> p h d", d=DH),
                                 r[:, nq:].broadcast_to([P, KH, DH]), ALU.mult).then_inc(qn_done, 1)

            def x_low(nb):
                wait(ve, xt_copied, nb + 1)
                wait(ve, pj_done, 16 * nb)
                ve.scalar_tensor_tensor(out=xT_lo[:], in0=bank[0][:], scalar=X_SCALE, in1=xT_hi[:],
                                        op0=ALU.mult, op1=ALU.subtract).then_inc(xlo_copied, 1)

            def split_p(b, h):
                q = KH * b + h
                wait(ve, mask_done, 3 * (q + 1))
                wait(ve, av_done, q)
                ve.tensor_copy(p_hi[:], prob[h % 2][:]).then_inc(phi_done, 1)
                wait(ve, phi_done, q + 1)
                ve.tensor_tensor(p_lo[:, 0:P_DVE], prob[h % 2][:, 0:P_DVE], p_hi[:, 0:P_DVE], ALU.subtract)\
                  .then_inc(plo_done, 1)

            def split_k(nb, t):
                n = T * nb + t
                k = kn[:].rearrange("p (h d) -> p h d", d=DH)
                wait(ve, qn_done, 2 * n + 2)
                wait(ve, tr_done, TR * (n - 1))
                ve.tensor_copy(ks[t % 2][:, :, 0], k).then_inc(hi_done, 1)
                wait(ve, hi_done, 3 * n + 1)
                ve.tensor_copy(ks[t % 2][:, :, 2], ks[t % 2][:, :, 0]).then_inc(hi_done, 1)
                ve.tensor_tensor(ks[t % 2][:, :, 1], k, ks[t % 2][:, :, 0], ALU.subtract)\
                  .then_inc(lo_done, 1)

            def split_q(nb, t):
                n = T * nb + t
                q = qn[:].rearrange("p (h d) -> p h d", d=DH)
                wait(ve, qg_done, n + 1)
                ve.tensor_copy(qs[t % 2][:, :, 0], q).then_inc(hi_done, 1)
                wait(ve, hi_done, 3 * n + 3)
                ve.tensor_tensor(qs[t % 2][:, :, 1], q, qs[t % 2][:, :, 0], ALU.subtract)\
                  .then_inc(lo_done, 1)

            def weigh(b, par, h):
                q = KH * b + h
                wait(ve, av_done, q + 1)
                wait(ve, og_done, q)
                ve.reciprocal(rden[:], acc_o[:, :, :, DH]).then_inc(rden_done, 1)
                wait(ve, rden_done, q + 1)
                wait(ve, o_done, q)
                ve.tensor_tensor(og[:], acc_o[:, :, :, 0:DH],
                                 rden[:].rearrange("p g (t o) -> p g t o", o=1).broadcast_to([P, G, T, DH]),
                                 ALU.mult).then_inc(og_done, 1)
                wait(ve, og_done, q + 1)
                if h == 0:
                    wait(ve, ot_done, T * b)
                ve.tensor_tensor(otok[:, :, h * DH:(h + 1) * DH], og[:, 0], og[:, 1], ALU.add)\
                  .then_inc(o_done, 1)

            def attn_stats(p):
                wait(ve, op_copied, p + 1)
                stats(1, p, attn, ln[0][0], ln[0][1])

            def attn_norm(p):
                wait(ve, rs_done[1], p + 1)
                wait(ve, res_free, 16 * (p + 1))
                apply(z2, attn, ln[0][1], ln[0][3], z2_done)

            def mix_norm(p):
                wait(ve, x1_done, p + 1)
                wait(ve, rs_done[2], p + 1)
                apply(xn3, x1, ln[1][1], ln[1][3], xn3_done)

            def y_norm(p):
                wait(ve, rs_done[3], p + 1)
                apply(z4, y, ln[2][1], ln[2][3], z4_done)

            def x1_stats(p):
                wait(ve, x1_done, p + 1)
                stats(2, p, x1, ln[1][0], ln[1][1])

            def y_stats(p):
                wait(ve, y_done, p + 1)
                stats(3, p, y, ln[2][0], ln[2][1])

            def iteration(b, par, prep, post, ahead):
                nb = b + 1
                for h in range(KH):
                    if prep and h == 0:
                        x_low(nb)
                    if ahead and h == 7:
                        stats_first(b + 2, par)
                    if prep and h in SPLIT_AT:
                        norm_qk(nb, SPLIT_AT[h])
                    if h >= 2:
                        weigh(b, par, h - 2)
                    elif post:
                        weigh(b - 1, 1 - par, KH - 2 + h)
                    if h >= 1:
                        split_p(b, h - 1)
                    elif post:
                        split_p(b - 1, KH - 1)
                    if post and h == 7:
                        y_stats(b - 1)
                    if ahead and h == 7:
                        norm_first(b + 2, par)
                    if post and h == 4:
                        attn_norm(b - 1)
                    if post and h == 5:
                        mix_norm(b - 1)
                    if post and h == 7:
                        y_norm(b - 1)
                    if prep and h in SPLIT_AT:
                        split_k(nb, SPLIT_AT[h])
                        split_q(nb, SPLIT_AT[h])
                    if post and h == 3:
                        attn_stats(b - 1)
                    if prep and h in SQUARES_AT:
                        sum_squares(nb, SQUARES_AT[h])
                    if prep and h in (1, 4):
                        inverse_norms(nb, h // 4)
                    if post and h == 4:
                        x1_stats(b - 1)

            ve.wait_ge(s_const, 8)
            stats_first(0, 0)
            setup()
            x_low(0)
            setup_rest()
            for m in range(2):
                sum_squares(0, 2 * m)
                sum_squares(0, 2 * m + 1)
                inverse_norms(0, m)
                for t in (2 * m, 2 * m + 1):
                    norm_qk(0, t)
                    split_k(0, t)
                    split_q(0, t)
            stats_first(1, 1)
            norm_first(1, 1)
            batches(ve, iteration)
            weigh(B - 1, (B - 1) % 2, KH - 2)
            split_p(B - 1, KH - 1)
            weigh(B - 1, (B - 1) % 2, KH - 1)
            attn_stats(B - 1)
            attn_norm(B - 1)
            x1_stats(B - 1)
            mix_norm(B - 1)
            y_stats(B - 1)
            y_norm(B - 1)


_INS = ["L0_attn_tokens", "L0_attn_norm_w", "L0_attn_Wq", "L0_attn_Wkv", "L0_attn_Wout",
        "L0_attn_q_gamma", "L0_attn_k_gamma", "L0_ffn_w_freq_real", "L0_ffn_w_freq_imag", "L0_ffn_bias"]


def kernel(**inputs):
    import numpy as _np
    import concourse.bacc as _bacc
    from concourse import mybir as _mybir
    from concourse.bass_utils import run_bass_kernel_spmd as _run

    nc = _bacc.Bacc("TRN2", target_bir_lowering=False, num_devices=1)
    arrays, args = {}, []
    for name in _INS:
        a = _np.ascontiguousarray(inputs[name])
        arrays[f"in_{name}_dram"] = a
        args.append(nc.dram_tensor(f"in_{name}_dram", a.shape, _mybir.dt.from_np(a.dtype), kind="ExternalInput").ap())
    angle = 2 * _np.pi / 128 * (_np.outer(_np.arange(128), _np.arange(128)) % 128)
    table = _np.stack([_np.cos(angle), _np.sin(angle), -_np.sin(angle)]).astype(_np.float32)
    arrays["dft_dram"] = table
    args.append(nc.dram_tensor("dft_dram", table.shape, _mybir.dt.float32, kind="ExternalInput").ap())
    o = nc.dram_tensor("out_0_dram", (8, 512, 128), _mybir.dt.float32, kind="ExternalOutput").ap()
    build(nc, *args, o)
    r = _run(nc, [arrays], core_ids=[0])
    return r.results[0]["out_0_dram"]
```
